# Optimizing a Trainium2 kernel written in Bass

```python
import numpy as np
import jax
import jax.numpy as jnp

def _softmax(x, axis=-1):
    return jax.nn.softmax(x, axis=axis)

def _gelu(x):
    return jax.nn.gelu(x, approximate=True)

def _silu(x):
    return jax.nn.silu(x)

def _sigmoid(x):
    return jax.nn.sigmoid(x)

def _layernorm(x, axis=-1, eps=1e-05):
    m = jnp.mean(x, axis=axis, keepdims=True)
    v = jnp.var(x, axis=axis, keepdims=True)
    return (x - m) / jnp.sqrt(v + eps)

def _scatter_add(tgt, idx, src, axis=0):
    return tgt.at[idx].add(src)

def _segment_sum(src, seg, n):
    return jax.ops.segment_sum(src, seg, n)
kernel_name = 'mk_decoder_preln_d2_seqx_r8_edf5b8'

def setup_inputs(seed: int=0):
    np.random.seed(seed)
    _w = jnp.asarray

    def _rec_inputs():
        import jax
        import jax.numpy as jnp
        _rk = jax.random.key(seed)
        x = -0.0002928 + 1 * jax.random.normal(jax.random.fold_in(_rk, 1), (64, 64, 128), jnp.float32)
        _lenS = 64 - jax.random.randint(jax.random.fold_in(_rk, 7), (64,), 0, max(1, 64 // 4) + 1, jnp.int32)
        _lenS2 = 64 - jax.random.randint(jax.random.fold_in(_rk, 8), (64,), 0, max(1, 64 // 4) + 1, jnp.int32)
        _ctx_1024P = jax.random.normal(jax.random.fold_in(_rk, 11), (64, 16, 128), jnp.float32)
        _ctx_1024c = jax.random.dirichlet(jax.random.fold_in(_rk, 511), 0.3 * jnp.ones((16,), jnp.float32), (64, 64))
        _ctx_1024t = jnp.einsum('bsk,bkd->bsd', _ctx_1024c, _ctx_1024P)
        _ctx_1024t = _ctx_1024t * jax.lax.rsqrt(jnp.mean(jnp.square(_ctx_1024t)) + 1e-12) * 0.953939
        ctx_1024 = -1.39393e-06 + 0.999914 * (_ctx_1024t + 0.3 * jax.random.normal(jax.random.fold_in(_rk, 611), (64, 64, 128), jnp.float32))
        return (x, ctx_1024)
    x, ctx_1024 = _rec_inputs()

    def _L0_attn_setup():
        import jax, jax.numpy as jnp
        import numpy as np
        D_MODEL = 128
        NUM_HEADS = 16
        HEAD_DIM = D_MODEL // NUM_HEADS
        MAX_SEQ_LEN = 256

        def _rope_tables(seq_len, head_dim):
            inv_freq = 1.0 / 10000.0 ** (jnp.arange(0, head_dim, 2, dtype=jnp.float32) / head_dim)
            pos = jnp.arange(seq_len, dtype=jnp.float32)
            freqs = jnp.einsum('i,j->ij', pos, inv_freq)
            return (jnp.cos(freqs), jnp.sin(freqs))

        def _apply_rope(x, cos_half, sin_half):
            x_even = x[..., ::2]
            x_odd = x[..., 1::2]
            rot_even = x_even * cos_half - x_odd * sin_half
            rot_odd = x_even * sin_half + x_odd * cos_half
            return jnp.stack([rot_even, rot_odd], axis=-1).reshape(x.shape)
        key = jax.random.key(seed)
        ks = jax.random.split(key, 9)
        B, S = (2, 256)
        glorot = lambda k: jax.random.normal(k, (D_MODEL, D_MODEL), dtype=jnp.float32) * (1.0 / np.sqrt(D_MODEL))
        return {'x': jax.random.normal(ks[0], (B, S, D_MODEL), dtype=jnp.float32), 'wq': glorot(ks[1]), 'bq': jnp.zeros((D_MODEL,), jnp.float32), 'wk': glorot(ks[2]), 'bk': jnp.zeros((D_MODEL,), jnp.float32), 'wv': glorot(ks[3]), 'bv': jnp.zeros((D_MODEL,), jnp.float32), 'wo': glorot(ks[4]), 'bo': jnp.zeros((D_MODEL,), jnp.float32)}
    _L0_attn_all = _L0_attn_setup()
    _L0_attn_in = {k: v for k, v in _L0_attn_all.items() if k in ('wq', 'bq', 'wk', 'bk', 'wv', 'bv', 'wo', 'bo')}
    del _L0_attn_all

    def _L0_xattn_setup():
        import jax, jax.numpy as jnp
        import numpy as np
        B, S, H, NH = (2, 256, 128, 4)
        DH = H // NH
        EPS = 1e-06

        def _parallel_stabilized(qh, kh, vh, ig, fg):
            log_fg = jax.nn.log_sigmoid(fg)
            cs = jnp.cumsum(log_fg, axis=2)
            ltr = jnp.tril(jnp.ones((qh.shape[2], qh.shape[2]), dtype=bool))
            log_fg_mat = jnp.where(ltr, cs - jnp.swapaxes(cs, 2, 3), -jnp.inf)
            log_D = log_fg_mat + jnp.swapaxes(ig, 2, 3)
            max_log_D = jnp.max(log_D, axis=-1, keepdims=True)
            D = jnp.exp(log_D - max_log_D)
            qk = jnp.einsum('bhsd,bhtd->bhst', qh, kh) / jnp.sqrt(jnp.float32(DH))
            C = qk * D
            normalizer = jnp.maximum(jnp.abs(jnp.sum(C, axis=-1, keepdims=True)), jnp.exp(-max_log_D))
            return jnp.einsum('bhst,bhtd->bhsd', C / (normalizer + EPS), vh)
        key = jax.random.key(seed)
        ks = jax.random.split(key, 6)
        q = jax.random.normal(ks[0], (B, S, H), dtype=jnp.float32)
        k = jax.random.normal(ks[1], (B, S, H), dtype=jnp.float32)
        v = jax.random.normal(ks[2], (B, S, H), dtype=jnp.float32)
        igate_kernel = jax.random.normal(ks[3], (3 * H, NH), dtype=jnp.float32) * 0.02
        fgate_kernel = jax.random.normal(ks[4], (3 * H, NH), dtype=jnp.float32) * 0.02
        igate_bias = jax.random.normal(ks[5], (NH,), dtype=jnp.float32) * 0.1
        fgate_bias = jnp.linspace(3.0, 6.0, NH, dtype=jnp.float32)
        outnorm_scale = jnp.ones((H,), dtype=jnp.float32)
        return {'q': q, 'k': k, 'v': v, 'igate_kernel': igate_kernel, 'igate_bias': igate_bias, 'fgate_kernel': fgate_kernel, 'fgate_bias': fgate_bias, 'outnorm_scale': outnorm_scale}
    _L0_xattn_all = _L0_xattn_setup()
    _L0_xattn_in = {k: v for k, v in _L0_xattn_all.items() if k in ('igate_kernel', 'igate_bias', 'fgate_kernel', 'fgate_bias', 'outnorm_scale')}
    del _L0_xattn_all

    def _L0_ffn_setup():
        import jax, jax.numpy as jnp
        import numpy as np
        D_MODEL = 128
        D_FF = 512
        NUM_M = 2
        E_ROUTER = 8 * NUM_M - 1
        D_FF_R = D_FF // NUM_M
        TOP_K = NUM_M * 2 - 1
        B, T = (2, 256)

        def _expert_stack(x, W1, b1, W2, b2):
            h = jax.nn.gelu(jnp.einsum('btd,edf->ebtf', x, W1) + b1[:, None, None, :], approximate=False)
            return jnp.einsum('ebtf,efd->ebtd', h, W2) + b2[:, None, None, :]
        key = jax.random.key(seed)
        ks = jax.random.split(key, 12)
        s = lambda fan_in: 1.0 / np.sqrt(fan_in)
        x = jax.random.normal(ks[0], (B, T, D_MODEL), dtype=jnp.float32)
        sW1 = jax.random.uniform(ks[1], (1, D_MODEL, D_FF), jnp.float32, -s(D_MODEL), s(D_MODEL))
        sb1 = jax.random.uniform(ks[2], (1, D_FF), jnp.float32, -s(D_MODEL), s(D_MODEL))
        sW2 = jax.random.uniform(ks[3], (1, D_FF, D_MODEL), jnp.float32, -s(D_FF), s(D_FF))
        sb2 = jax.random.uniform(ks[4], (1, D_MODEL), jnp.float32, -s(D_FF), s(D_FF))
        rW1 = jax.random.uniform(ks[5], (E_ROUTER, D_MODEL, D_FF_R), jnp.float32, -s(D_MODEL), s(D_MODEL))
        rb1 = jax.random.uniform(ks[6], (E_ROUTER, D_FF_R), jnp.float32, -s(D_MODEL), s(D_MODEL))
        rW2 = jax.random.uniform(ks[7], (E_ROUTER, D_FF_R, D_MODEL), jnp.float32, -s(D_FF_R), s(D_FF_R))
        rb2 = jax.random.uniform(ks[8], (E_ROUTER, D_MODEL), jnp.float32, -s(D_FF_R), s(D_FF_R))
        gW = jax.random.uniform(ks[9], (D_MODEL, E_ROUTER), jnp.float32, -s(D_MODEL), s(D_MODEL))
        gb = jax.random.uniform(ks[10], (E_ROUTER,), jnp.float32, -s(D_MODEL), s(D_MODEL))
        return {'x': x, 'sW1': sW1, 'sb1': sb1, 'sW2': sW2, 'sb2': sb2, 'rW1': rW1, 'rb1': rb1, 'rW2': rW2, 'rb2': rb2, 'gW': gW, 'gb': gb}
    _L0_ffn_all = _L0_ffn_setup()
    _L0_ffn_in = {k: v for k, v in _L0_ffn_all.items() if k in ('sW1', 'sb1', 'sW2', 'sb2', 'rW1', 'rb1', 'rW2', 'rb2', 'gW', 'gb')}
    del _L0_ffn_all

    def _L1_attn_setup():
        import jax, jax.numpy as jnp
        import numpy as np
        B, T, D_MODEL, N_HEADS = (2, 256, 128, 16)
        key = jax.random.key(seed)
        ks = jax.random.split(key, 5)
        w_scale = 0.02
        return {'x': jax.random.normal(ks[0], (B, T, D_MODEL), jnp.float32), 'Wq': jax.random.normal(ks[1], (D_MODEL, D_MODEL), jnp.float32) * w_scale, 'Wk': jax.random.normal(ks[2], (D_MODEL, D_MODEL), jnp.float32) * w_scale, 'Wv': jax.random.normal(ks[3], (D_MODEL, D_MODEL), jnp.float32) * w_scale, 'Wo': jax.random.normal(ks[4], (D_MODEL, D_MODEL), jnp.float32) * w_scale}
    _L1_attn_all = _L1_attn_setup()
    _L1_attn_in = {k: v for k, v in _L1_attn_all.items() if k in ('Wq', 'Wk', 'Wv', 'Wo')}
    del _L1_attn_all

    def _L1_xattn_setup():
        import jax, jax.numpy as jnp
        import numpy as np
        DIM = 128
        HEAD_DIM = 64
        NUM_HEADS = 8
        INNER = HEAD_DIM * NUM_HEADS
        ROT_DIM = HEAD_DIM
        ROPE_BASE = 10000.0
        EPS = 1e-05

        def layer_norm(x, g, b):
            mu = jnp.mean(x, axis=-1, keepdims=True)
            var = jnp.var(x, axis=-1, keepdims=True)
            return (x - mu) * jax.lax.rsqrt(var + EPS) * g + b

        def rope_rotate_k(k):
            n = k.shape[1]
            half = ROT_DIM // 2
            inv_freq = 1.0 / ROPE_BASE ** (jnp.arange(0, ROT_DIM, 2, dtype=jnp.float32) / ROT_DIM)
            theta = jnp.arange(n, dtype=jnp.float32)[:, None] * inv_freq[None, :]
            angles = jnp.concatenate([theta, theta], axis=-1)
            cos = jnp.cos(angles)[None, :, None, :].astype(k.dtype)
            sin = jnp.sin(angles)[None, :, None, :].astype(k.dtype)
            k_rope, k_pass = (k[..., :ROT_DIM], k[..., ROT_DIM:])
            neg_half = jnp.concatenate([-k_rope[..., half:], k_rope[..., :half]], axis=-1)
            k_rope = k_rope * cos + neg_half * sin
            return jnp.concatenate([k_rope, k_pass], axis=-1)
        key = jax.random.key(seed)
        ks = jax.random.split(key, 5)
        b, n, m = (8, 1024, 64)
        s = 1.0 / np.sqrt(DIM)
        return {'x': jax.random.normal(ks[0], (b, n, DIM), jnp.float32), 'latents': jax.random.normal(ks[1], (b, m, DIM), jnp.float32), 'gamma_x': jnp.ones((DIM,), jnp.float32), 'beta_x': jnp.zeros((DIM,), jnp.float32), 'gamma_l': jnp.ones((DIM,), jnp.float32), 'beta_l': jnp.zeros((DIM,), jnp.float32), 'Wq': jax.random.normal(ks[2], (DIM, INNER), jnp.float32) * s, 'Wkv': jax.random.normal(ks[3], (DIM, 2 * INNER), jnp.float32) * s, 'Wo': jax.random.normal(ks[4], (INNER, DIM), jnp.float32) * (1.0 / np.sqrt(INNER))}
    _L1_xattn_all = _L1_xattn_setup()
    _L1_xattn_in = {k: v for k, v in _L1_xattn_all.items() if k in ('gamma_x', 'beta_x', 'gamma_l', 'beta_l', 'Wq', 'Wkv', 'Wo')}
    del _L1_xattn_all

    def _L1_ffn_setup():
        import jax, jax.numpy as jnp
        import numpy as np
        B, M, D = (4, 256, 128)
        N, P = (64, 32)
        key = jax.random.key(seed)
        k1, k2, k3, k4 = jax.random.split(key, 4)
        x = jax.random.normal(k1, (B, M, D), dtype=jnp.float32)
        phi = jax.random.normal(k2, (D, N, P), dtype=jnp.float32) * (1.0 / np.sqrt(D))
        W = jax.random.normal(k3, (N, D, D), dtype=jnp.float32) * (1.0 / np.sqrt(D))
        b = jax.random.normal(k4, (N, D), dtype=jnp.float32) * 0.01
        return {'x': x, 'phi': phi, 'W': W, 'b': b}
    _L1_ffn_all = _L1_ffn_setup()
    _L1_ffn_in = {k: v for k, v in _L1_ffn_all.items() if k in ('phi', 'W', 'b')}
    del _L1_ffn_all
    return {'x': x, 'ctx_1024': ctx_1024, 'L0_attn_wq': _L0_attn_in['wq'], 'L0_attn_bq': _L0_attn_in['bq'], 'L0_attn_wk': _L0_attn_in['wk'], 'L0_attn_bk': _L0_attn_in['bk'], 'L0_attn_wv': _L0_attn_in['wv'], 'L0_attn_bv': _L0_attn_in['bv'], 'L0_attn_wo': _L0_attn_in['wo'], 'L0_attn_bo': _L0_attn_in['bo'], 'L0_xattn_igate_kernel': _L0_xattn_in['igate_kernel'], 'L0_xattn_igate_bias': _L0_xattn_in['igate_bias'], 'L0_xattn_fgate_kernel': _L0_xattn_in['fgate_kernel'], 'L0_xattn_fgate_bias': _L0_xattn_in['fgate_bias'], 'L0_xattn_outnorm_scale': _L0_xattn_in['outnorm_scale'], 'L0_ffn_sW1': _L0_ffn_in['sW1'], 'L0_ffn_sb1': _L0_ffn_in['sb1'], 'L0_ffn_sW2': _L0_ffn_in['sW2'], 'L0_ffn_sb2': _L0_ffn_in['sb2'], 'L0_ffn_rW1': _L0_ffn_in['rW1'], 'L0_ffn_rb1': _L0_ffn_in['rb1'], 'L0_ffn_rW2': _L0_ffn_in['rW2'], 'L0_ffn_rb2': _L0_ffn_in['rb2'], 'L0_ffn_gW': _L0_ffn_in['gW'], 'L0_ffn_gb': _L0_ffn_in['gb'], 'L1_attn_Wq': _L1_attn_in['Wq'], 'L1_attn_Wk': _L1_attn_in['Wk'], 'L1_attn_Wv': _L1_attn_in['Wv'], 'L1_attn_Wo': _L1_attn_in['Wo'], 'L1_xattn_gamma_x': _L1_xattn_in['gamma_x'], 'L1_xattn_beta_x': _L1_xattn_in['beta_x'], 'L1_xattn_gamma_l': _L1_xattn_in['gamma_l'], 'L1_xattn_beta_l': _L1_xattn_in['beta_l'], 'L1_xattn_Wq': _L1_xattn_in['Wq'], 'L1_xattn_Wkv': _L1_xattn_in['Wkv'], 'L1_xattn_Wo': _L1_xattn_in['Wo'], 'L1_ffn_phi': _L1_ffn_in['phi'], 'L1_ffn_W': _L1_ffn_in['W'], 'L1_ffn_b': _L1_ffn_in['b']}

def reference(x, ctx_1024, L0_attn_wq, L0_attn_bq, L0_attn_wk, L0_attn_bk, L0_attn_wv, L0_attn_bv, L0_attn_wo, L0_attn_bo, L0_xattn_igate_kernel, L0_xattn_igate_bias, L0_xattn_fgate_kernel, L0_xattn_fgate_bias, L0_xattn_outnorm_scale, L0_ffn_sW1, L0_ffn_sb1, L0_ffn_sW2, L0_ffn_sb2, L0_ffn_rW1, L0_ffn_rb1, L0_ffn_rW2, L0_ffn_rb2, L0_ffn_gW, L0_ffn_gb, L1_attn_Wq, L1_attn_Wk, L1_attn_Wv, L1_attn_Wo, L1_xattn_gamma_x, L1_xattn_beta_x, L1_xattn_gamma_l, L1_xattn_beta_l, L1_xattn_Wq, L1_xattn_Wkv, L1_xattn_Wo, L1_ffn_phi, L1_ffn_W, L1_ffn_b):
    import jax
    import jax.numpy as jnp

    def _L0_attn_ref(x, wq, bq, wk, bk, wv, bv, wo, bo):
        import jax, jax.numpy as jnp
        import numpy as np
        D_MODEL = 128
        NUM_HEADS = 16
        HEAD_DIM = D_MODEL // NUM_HEADS
        MAX_SEQ_LEN = 256

        def _rope_tables(seq_len, head_dim):
            inv_freq = 1.0 / 10000.0 ** (jnp.arange(0, head_dim, 2, dtype=jnp.float32) / head_dim)
            pos = jnp.arange(seq_len, dtype=jnp.float32)
            freqs = jnp.einsum('i,j->ij', pos, inv_freq)
            return (jnp.cos(freqs), jnp.sin(freqs))

        def _apply_rope(x, cos_half, sin_half):
            x_even = x[..., ::2]
            x_odd = x[..., 1::2]
            rot_even = x_even * cos_half - x_odd * sin_half
            rot_odd = x_even * sin_half + x_odd * cos_half
            return jnp.stack([rot_even, rot_odd], axis=-1).reshape(x.shape)
        B, S, _ = x.shape
        q = (x @ wq + bq).reshape(B, S, NUM_HEADS, HEAD_DIM)
        k = (x @ wk + bk).reshape(B, S, NUM_HEADS, HEAD_DIM)
        v = (x @ wv + bv).reshape(B, S, NUM_HEADS, HEAD_DIM)
        cos, sin = _rope_tables(S, HEAD_DIM)
        cos = cos[None, :, None, :]
        sin = sin[None, :, None, :]
        q = _apply_rope(q, cos, sin)
        k = _apply_rope(k, cos, sin)
        q = q.transpose(0, 2, 1, 3)
        k = k.transpose(0, 2, 1, 3)
        v = v.transpose(0, 2, 1, 3)
        scores = jnp.einsum('bhqd,bhkd->bhqk', q, k) / jnp.sqrt(jnp.float32(HEAD_DIM))
        causal = jnp.where(jnp.tril(jnp.ones((S, S), jnp.float32)) == 0, -1000000000.0, 0.0)
        scores = scores + causal
        attn = jax.nn.softmax(scores, axis=-1)
        out = jnp.einsum('bhqk,bhkd->bhqd', attn, v)
        out = out.transpose(0, 2, 1, 3).reshape(B, S, D_MODEL)
        return out @ wo + bo

    def _L0_xattn_ref(q, k, v, igate_kernel, igate_bias, fgate_kernel, fgate_bias, outnorm_scale):
        import jax, jax.numpy as jnp
        import numpy as np
        B, S, H, NH = (2, 256, 128, 4)
        DH = H // NH
        EPS = 1e-06

        def _parallel_stabilized(qh, kh, vh, ig, fg):
            log_fg = jax.nn.log_sigmoid(fg)
            cs = jnp.cumsum(log_fg, axis=2)
            ltr = jnp.tril(jnp.ones((qh.shape[2], qh.shape[2]), dtype=bool))
            log_fg_mat = jnp.where(ltr, cs - jnp.swapaxes(cs, 2, 3), -jnp.inf)
            log_D = log_fg_mat + jnp.swapaxes(ig, 2, 3)
            max_log_D = jnp.max(log_D, axis=-1, keepdims=True)
            D = jnp.exp(log_D - max_log_D)
            qk = jnp.einsum('bhsd,bhtd->bhst', qh, kh) / jnp.sqrt(jnp.float32(DH))
            C = qk * D
            normalizer = jnp.maximum(jnp.abs(jnp.sum(C, axis=-1, keepdims=True)), jnp.exp(-max_log_D))
            return jnp.einsum('bhst,bhtd->bhsd', C / (normalizer + EPS), vh)
        Bq, Sq, Hq = q.shape
        x = jnp.concatenate([q, k, v], axis=-1)
        ig = x @ igate_kernel + igate_bias
        fg = x @ fgate_kernel + fgate_bias
        ig = jnp.transpose(ig, (0, 2, 1))[..., None]
        fg = jnp.transpose(fg, (0, 2, 1))[..., None]
        qh = jnp.transpose(q.reshape(Bq, Sq, NH, DH), (0, 2, 1, 3))
        kh = jnp.transpose(k.reshape(Bq, Sq, NH, DH), (0, 2, 1, 3))
        vh = jnp.transpose(v.reshape(Bq, Sq, NH, DH), (0, 2, 1, 3))
        h = _parallel_stabilized(qh, kh, vh, ig, fg)
        mean = jnp.mean(h, axis=-1, keepdims=True)
        var = jnp.mean((h - mean) ** 2, axis=-1, keepdims=True)
        h_norm = (h - mean) * jax.lax.rsqrt(var + 1e-05)
        h_norm = h_norm * outnorm_scale.reshape(1, NH, 1, DH)
        out = jnp.transpose(h_norm, (0, 2, 1, 3)).reshape(Bq, Sq, Hq)
        return out

    def _L0_ffn_ref(x, sW1, sb1, sW2, sb2, rW1, rb1, rW2, rb2, gW, gb):
        import jax, jax.numpy as jnp
        import numpy as np
        D_MODEL = 128
        D_FF = 512
        NUM_M = 2
        E_ROUTER = 8 * NUM_M - 1
        D_FF_R = D_FF // NUM_M
        TOP_K = NUM_M * 2 - 1
        B, T = (2, 256)

        def _expert_stack(x, W1, b1, W2, b2):
            h = jax.nn.gelu(jnp.einsum('btd,edf->ebtf', x, W1) + b1[:, None, None, :], approximate=False)
            return jnp.einsum('ebtf,efd->ebtd', h, W2) + b2[:, None, None, :]
        shared_enc = _expert_stack(x, sW1, sb1, sW2, sb2).sum(0)
        weights = jax.nn.softmax(x @ gW + gb, axis=-1)
        topv, topi = jax.lax.top_k(weights, TOP_K)
        gated = (jax.nn.one_hot(topi, E_ROUTER, dtype=weights.dtype) * topv[..., None]).sum(axis=-2)
        router_out = _expert_stack(x, rW1, rb1, rW2, rb2)
        router_enc = jnp.einsum('ebtd,bte->btd', router_out, gated)
        return shared_enc + router_enc + x

    def _L1_attn_ref(x, Wq, Wk, Wv, Wo):
        import jax, jax.numpy as jnp
        import numpy as np
        B, T, D_MODEL, N_HEADS = (2, 256, 128, 16)
        Bv, Tv, _ = x.shape
        H = N_HEADS
        D = D_MODEL // H
        q = (x @ Wq.T).reshape(Bv, Tv, H, D).transpose(0, 2, 1, 3)
        k = (x @ Wk.T).reshape(Bv, Tv, H, D).transpose(0, 2, 1, 3)
        v = (x @ Wv.T).reshape(Bv, Tv, H, D).transpose(0, 2, 1, 3)
        scale = jnp.sqrt(jnp.asarray(D, jnp.float32))
        scores = jnp.einsum('bhqd,bhkd->bhqk', q, k) / scale
        slopes = jnp.asarray([2.0 ** (-8.0 * h / H) for h in range(1, H + 1)], jnp.float32)
        pos = jnp.arange(Tv)
        dist = jnp.abs(pos[None, :] - pos[:, None]).astype(jnp.float32)
        bias = -dist[None, :, :] * slopes[:, None, None]
        causal_mask = jnp.triu(jnp.ones((Tv, Tv), dtype=bool), 1)
        bias = jnp.where(causal_mask[None, :, :], -jnp.inf, bias)
        scores = scores + bias[None]
        attn = jax.nn.softmax(scores, axis=-1)
        out = jnp.einsum('bhqk,bhkd->bhqd', attn, v)
        out = out.transpose(0, 2, 1, 3).reshape(Bv, Tv, D_MODEL)
        return out @ Wo.T

    def _L1_xattn_ref(x, latents, gamma_x, beta_x, gamma_l, beta_l, Wq, Wkv, Wo):
        import jax, jax.numpy as jnp
        import numpy as np
        DIM = 128
        HEAD_DIM = 64
        NUM_HEADS = 8
        INNER = HEAD_DIM * NUM_HEADS
        ROT_DIM = HEAD_DIM
        ROPE_BASE = 10000.0
        EPS = 1e-05

        def layer_norm(x, g, b):
            mu = jnp.mean(x, axis=-1, keepdims=True)
            var = jnp.var(x, axis=-1, keepdims=True)
            return (x - mu) * jax.lax.rsqrt(var + EPS) * g + b

        def rope_rotate_k(k):
            n = k.shape[1]
            half = ROT_DIM // 2
            inv_freq = 1.0 / ROPE_BASE ** (jnp.arange(0, ROT_DIM, 2, dtype=jnp.float32) / ROT_DIM)
            theta = jnp.arange(n, dtype=jnp.float32)[:, None] * inv_freq[None, :]
            angles = jnp.concatenate([theta, theta], axis=-1)
            cos = jnp.cos(angles)[None, :, None, :].astype(k.dtype)
            sin = jnp.sin(angles)[None, :, None, :].astype(k.dtype)
            k_rope, k_pass = (k[..., :ROT_DIM], k[..., ROT_DIM:])
            neg_half = jnp.concatenate([-k_rope[..., half:], k_rope[..., :half]], axis=-1)
            k_rope = k_rope * cos + neg_half * sin
            return jnp.concatenate([k_rope, k_pass], axis=-1)
        b, n, _ = x.shape
        m = latents.shape[1]
        h, d = (NUM_HEADS, HEAD_DIM)
        scale = d ** (-0.5)
        xn = layer_norm(x, gamma_x, beta_x)
        ln = layer_norm(latents, gamma_l, beta_l)
        q = (ln @ Wq).reshape(b, m, h, d)
        kv_x = xn @ Wkv
        k_x, v_x = (kv_x[..., :INNER], kv_x[..., INNER:])
        kv_l = ln @ Wkv
        k_l, v_l = (kv_l[..., :INNER], kv_l[..., INNER:])
        k_x = k_x.reshape(b, n, h, d)
        v_x = v_x.reshape(b, n, h, d)
        k_x = rope_rotate_k(k_x)
        q = jnp.transpose(q, (0, 2, 1, 3)) * scale
        k_x = jnp.transpose(k_x, (0, 2, 1, 3))
        v_x = jnp.transpose(v_x, (0, 2, 1, 3))
        k_l = jnp.transpose(k_l.reshape(b, m, h, d), (0, 2, 1, 3))
        v_l = jnp.transpose(v_l.reshape(b, m, h, d), (0, 2, 1, 3))
        k = jnp.concatenate([k_x, k_l], axis=2)
        v = jnp.concatenate([v_x, v_l], axis=2)
        sim = jnp.einsum('bhid,bhjd->bhij', q, k)
        attn = jax.nn.softmax(sim, axis=-1)
        out = jnp.einsum('bhij,bhjd->bhid', attn, v)
        out = jnp.transpose(out, (0, 2, 1, 3)).reshape(b, m, INNER)
        return out @ Wo

    def _L1_ffn_ref(x, phi, W, b):
        import jax, jax.numpy as jnp
        import numpy as np
        B, M, D = (4, 256, 128)
        N, P = (64, 32)
        logits = jnp.einsum('bmd,dnp->bmnp', x, phi)
        dispatch = jax.nn.softmax(logits, axis=0)
        bsz, m, n, p = logits.shape
        combine = jax.nn.softmax(logits.reshape(bsz, m, n * p), axis=-1).reshape(bsz, m, n, p)
        slots = jnp.einsum('bmd,bmnp->bnpd', x, dispatch)
        y = jnp.einsum('bnpd,nde->bnpe', slots, W) + b[None, :, None, :]
        out = jnp.einsum('bnpd,bmnp->bmd', y, combine)
        return out
    x = x + _L0_attn_ref(_layernorm(x, axis=-1), L0_attn_wq, L0_attn_bq, L0_attn_wk, L0_attn_bk, L0_attn_wv, L0_attn_bv, L0_attn_wo, L0_attn_bo)
    x = x + _L0_xattn_ref(_layernorm(x, axis=-1), ctx_1024, ctx_1024, L0_xattn_igate_kernel, L0_xattn_igate_bias, L0_xattn_fgate_kernel, L0_xattn_fgate_bias, L0_xattn_outnorm_scale)
    x = x + _L0_ffn_ref(_layernorm(x, axis=-1), L0_ffn_sW1, L0_ffn_sb1, L0_ffn_sW2, L0_ffn_sb2, L0_ffn_rW1, L0_ffn_rb1, L0_ffn_rW2, L0_ffn_rb2, L0_ffn_gW, L0_ffn_gb)
    x = x + _L1_attn_ref(_layernorm(x, axis=-1), L1_attn_Wq, L1_attn_Wk, L1_attn_Wv, L1_attn_Wo)
    x = x + _L1_xattn_ref(ctx_1024, _layernorm(x, axis=-1), L1_xattn_gamma_x, L1_xattn_beta_x, L1_xattn_gamma_l, L1_xattn_beta_l, L1_xattn_Wq, L1_xattn_Wkv, L1_xattn_Wo)
    x = x + _L1_ffn_ref(_layernorm(x, axis=-1), L1_ffn_phi, L1_ffn_W, L1_ffn_b)
    return x

_drawn_inputs = setup_inputs


def setup_inputs(seed=0):
    import zlib

    import numpy as np

    out = dict(_drawn_inputs(seed))
    spreads = {'L0_attn_bq': (0.0, 0.31),
     'L0_attn_bk': (0.0, 0.449),
     'L0_attn_bv': (0.0, 0.1),
     'L0_attn_bo': (0.0, 0.1),
     'L0_xattn_outnorm_scale': (1.0, 0.2),
     'L1_xattn_gamma_x': (1.0, 0.6),
     'L1_xattn_beta_x': (0.0, 0.426),
     'L1_xattn_gamma_l': (1.0, 0.6),
     'L1_xattn_beta_l': (0.0, 0.411)}
    factors = {'L0_xattn_igate_bias': 64.0,
     'L0_xattn_fgate_kernel': 5.051,
     'L0_ffn_sb1': 8.0,
     'L0_ffn_sb2': 5.793,
     'L0_ffn_rW1': 3.685,
     'L0_ffn_rb1': 8.0,
     'L0_ffn_rW2': 3.467,
     'L0_ffn_rb2': 8.0,
     'L0_ffn_gW': 3.789,
     'L0_ffn_gb': 8.0,
     'L1_attn_Wq': 8.0,
     'L1_attn_Wk': 8.0,
     'L1_attn_Wv': 7.19,
     'L1_attn_Wo': 7.165,
     'L1_ffn_phi': 8.0,
     'L1_ffn_W': 4.124,
     'L1_ffn_b': 53.382}
    for name, (base, spread) in spreads.items():
        noise = np.random.default_rng([zlib.crc32(name.encode()), seed]).standard_normal(out[name].shape)
        drawn = base * np.exp(spread * noise) if base else spread * noise
        out[name] = jnp.asarray(drawn.astype(out[name].dtype))
    for name, factor in factors.items():
        out[name] = (out[name] * factor).astype(out[name].dtype)
    return out
```

```python
from contextlib import ExitStack

import numpy as np
import concourse.bass as bass
from concourse import mybir
from concourse.alu_op_type import AluOpType as ALU

ACT = mybir.ActivationFunctionType
F32 = mybir.dt.float32
BF16 = mybir.dt.bfloat16
AX = mybir.AxisListType.X

P = 128
B, S, D = 64, 64, 128
NT = B * S // P
PER = P // S
LN_EPS = 1e-5
GATES = 64


def has(k, n=NT):
    return not isinstance(k, int) or 0 <= k < n


def turns(eng, turn, first, last, ring, n=NT, head=1, tail=1):
    for t in range(first, head * ring):
        turn(t, t % ring)
    with eng.Fori(head, n // ring - tail) as i:
        for u in range(ring):
            turn(i * ring + u, u)
    for t in range(n - tail * ring, last):
        turn(t, t % ring)


USED = []


def clear_semaphores(nc):
    with nc.Block() as block:
        @block.sync
        def _(sync):
            sync.sem_clear(range(min(USED), max(USED) + 1))
    USED.clear()


class Mem:

    def __init__(self, nc, tag):
        self.nc, self.tag, self.stack = nc, tag, ExitStack()

    def __enter__(self):
        self.stack.__enter__()
        return self

    def __exit__(self, *a):
        return self.stack.__exit__(*a)

    def sb(self, name, shape, dt=F32):
        return self.stack.enter_context(self.nc.sbuf_tensor(f"{self.tag}_{name}", shape, dt))

    def ps(self, name, shape=(P, 512), dt=F32):
        return self.stack.enter_context(self.nc.psum_tensor(f"{self.tag}_{name}", list(shape), dt))

    def sem(self, name):
        s = self.stack.enter_context(self.nc.semaphore(f"{self.tag}_{name}"))
        USED.append(s.num)
        return s

    def sems(self, name, n):
        return [self.sem(f"{name}{i}") for i in range(n)]


def carry(dve, g):
    g["carries"] = (g["carries"] + 1) % GATES
    dve.memset(g["gate"][:, g["carries"]:g["carries"] + 1], 0.0)


def row_bc(ap, n):
    p, m = ap.shape
    return ap.unsqueeze(1).to_broadcast([p, n, m])


def col_bc(ap, n):
    p, m = ap.shape
    return ap.unsqueeze(2).to_broadcast([p, m, n])


def load_and_norm(nc, g, io):
    R = 4
    x_d = io["x"].rearrange("(t b) s d -> t (b s) d", b=PER)
    c_d = io["ctx_1024"].rearrange("(t b) s d -> t (b s) d", b=PER)
    with Mem(nc, "ld") as m:
        ctx = m.sb("ctx", [P, R, D])
        stats = m.sb("stats", [P, R, 2, 6])
        mv = m.sb("mv", [P, R, 2, 2])
        rstd = m.sb("rstd", [P, R, 2])
        xn = m.sb("xn", [P, R, D])
        cn = m.sb("cn", [P, R, D])
        tp = [m.ps(f"tp{i}") for i in range(2)]
        consts_in, half_set = m.sem("consts_in"), m.sem("half_set")
        x_in, c_in = m.sems("x_in", R), m.sems("c_in", R)
        stats_made, moments, var_eps, rstd_made = m.sem("stats_made"), m.sem("moments"), m.sem("var_eps"), m.sem("rstd_made")
        normed, transposed, copied = m.sem("normed"), m.sem("transposed"), m.sem("copied")
        loads = [(g["ident"][:, :], io["c_ident"]), (g["gbx"][:, :], io["w_gbx"]), (g["gbl"][:, :], io["w_gbl"])]
        block = m.stack.enter_context(nc.Block())

        @block.sync
        def _(sync):
            for dst, src in loads:
                sync.dma_start(dst, src).then_inc(consts_in, 16)

        @block.vector
        def _(dve):
            dve.memset(g["neghalf"][:, :], -0.5).then_inc(half_set, 1)
            dve.memset(g["eps"][:, :], LN_EPS).then_inc(half_set, 1)

            def turn(t, u):
                k, v = t + 1, (u + 1) % R
                if has(k):
                    dve.wait_ge(x_in[v], (k // R + 1) * 16)
                    dve.wait_ge(c_in[v], (k // R + 1) * 16)
                    if has(k - R):
                        dve.wait_ge(rstd_made, k - R + 1)
                    dve.bn_stats(stats[:, v, 0, :], g["xs"][:, bass.ds(k, 1), :].rearrange("p a d -> p (a d)")).then_inc(stats_made, 1)
                    dve.bn_stats(stats[:, v, 1, :], ctx[:, v, :]).then_inc(stats_made, 1)
                    dve.wait_ge(stats_made, 2 * (k + 1))
                    carry(dve, g)
                    dve.bn_aggr(mv[:, v, 0, :], stats[:, v, 0, :]).then_inc(moments, 1)
                    dve.bn_aggr(mv[:, v, 1, :], stats[:, v, 1, :]).then_inc(moments, 1)
                if has(t):
                    dve.wait_ge(moments, 2 * (t + 1))
                    dve.wait_ge(rstd_made, t + 1)
                    if has(t - R):
                        dve.wait_ge(transposed, t - R + 1)
                    dve.tensor_scalar(xn[:, u, :], g["xs"][:, bass.ds(t, 1), :].rearrange("p a d -> p (a d)"),
                                      mv[:, u, 0, 0:1], rstd[:, u, 0:1], ALU.subtract, ALU.mult).then_inc(normed, 1)
                    dve.tensor_scalar(cn[:, u, :], ctx[:, u, :],
                                      mv[:, u, 1, 0:1], rstd[:, u, 1:2], ALU.subtract, ALU.mult).then_inc(normed, 1)

            turns(dve, turn, -1, NT, R)

        @block.gpsimd
        def _(pool):
            pool.wait_ge(half_set, 2)

            def turn(t, u):
                pool.wait_ge(moments, 2 * (t + 1))
                if has(t - R):
                    pool.wait_ge(normed, 2 * (t - R + 1))
                pool.tensor_tensor(rstd[:, u, :], mv[:, u, :, 1], g["eps"][:, 0:2], ALU.add).then_inc(var_eps, 1)
                pool.wait_ge(var_eps, t + 1)
                pool.tensor_tensor(rstd[:, u, :], rstd[:, u, :], g["neghalf"][:, 0:2], ALU.pow).then_inc(rstd_made, 1)

            turns(pool, turn, 0, NT, R)

        @block.tensor
        def _(pe):
            pe.wait_ge(consts_in, 16 * len(loads))

            def turn(t, u):
                pe.wait_ge(c_in[u], (t // R + 1) * 16)
                pe.wait_ge(normed, 2 * (t + 1))
                if has(t - 2):
                    pe.wait_ge(copied, 3 * (t - 1))
                bank = tp[u % 2]
                pe.transpose(bank[:, 0:P], xn[:, u, :], g["ident"][:, :])
                pe.transpose(bank[:, P:2 * P], ctx[:, u, :], g["ident"][:, :])
                pe.transpose(bank[:, 2 * P:3 * P], cn[:, u, :], g["ident"][:, :]).then_inc(transposed, 1)

            turns(pe, turn, 0, NT, R)

        @block.scalar
        def _(act):
            act.wait_ge(consts_in, 16 * len(loads))

            def load(t, u):
                act.dma_start(g["xs"][:, bass.ds(t, 1), :].rearrange("p a d -> p (a d)"),
                              x_d[bass.ds(t, 1), :, :].rearrange("a p d -> p (a d)")).then_inc(x_in[u], 16)
                act.dma_start(ctx[:, u, :],
                              c_d[bass.ds(t, 1), :, :].rearrange("a p d -> p (a d)")).then_inc(c_in[u], 16)

            for t in range(R - 1):
                load(t, t)

            def turn(t, u):
                if has(t + R - 1):
                    if has(t - 1):
                        act.wait_ge(transposed, t)
                        act.wait_ge(normed, 2 * t)
                    load(t + R - 1, (u + R - 1) % R)
                act.wait_ge(transposed, t + 1)
                bank = tp[u % 2]
                at = bass.ds(t * P, P)
                act.activation(g["xnT"][:, at], bank[:, 0:P], ACT.Copy).then_inc(copied, 1)
                act.activation(g["ctxT"][:, at], bank[:, P:2 * P], ACT.Copy).then_inc(copied, 1)
                act.activation(g["cnT"][:, at], bank[:, 2 * P:3 * P], ACT.Identity, bias=g["gbx"][:, 1:2],
                               scale=g["gbx"][:, 0:1]).then_inc(copied, 1)

            turns(act, turn, 0, NT, R)


class Norm:

    def __init__(self, m, g, levels, x_made, keep=False, rows=False):
        self.g, self.levels, self.x_made, self.keep, self.rows = g, levels, x_made, keep, rows
        self.kept = m.sem("n_kept")
        self.stats = m.sb("n_stats", [P, 2, levels, 6])
        self.mv = m.sb("n_mv", [P, 2, levels, 2])
        self.rstd = m.sb("n_rstd", [P, 2, levels])
        self.xn = m.sb("n_xn", [P, 2, levels, D])
        self.stats_made = m.sems("n_stats_made", levels)
        self.moments = m.sems("n_moments", levels)
        self.var_eps = m.sems("n_var_eps", levels)
        self.rstd_made = m.sems("n_rstd_made", levels)
        self.normed = m.sems("n_normed", levels)
        self.transposed = m.sem("n_transposed")
        self.copied = m.sem("n_copied")

    def dve_stats(self, dve, k, v, l=0, first=False):
        if l == 0:
            dve.wait_ge(self.x_made, k + 1)
            src = self.g["xs"][:, bass.ds(k, 1), :].rearrange("p a d -> p (a d)")
        else:
            dve.wait_ge(self.normed[0], k + 1)
            src = self.xn[:, v, 0, :]
        carry(dve, self.g)
        dve.bn_stats(self.stats[:, v, l, :], src).then_inc(self.stats_made[l], 1)
        if has(k - 2) and not first:
            dve.wait_ge(self.rstd_made[l], k - 1)
        dve.wait_ge(self.stats_made[l], k + 1)
        carry(dve, self.g)
        dve.bn_aggr(self.mv[:, v, l, :], self.stats[:, v, l, :]).then_inc(self.moments[l], 1)

    def pool_rstd(self, pool, k, v, l=0, first=False):
        if has(k - 2) and not first:
            pool.wait_ge(self.normed[l], k - 1)
        pool.wait_ge(self.moments[l], k + 1)
        pool.tensor_tensor(self.rstd[:, v, l:l + 1], self.mv[:, v, l, 1:2], self.g["eps"][:, 0:1],
                           ALU.add).then_inc(self.var_eps[l], 1)
        pool.wait_ge(self.var_eps[l], k + 1)
        pool.tensor_tensor(self.rstd[:, v, l:l + 1], self.rstd[:, v, l:l + 1], self.g["neghalf"][:, 0:1],
                           ALU.pow).then_inc(self.rstd_made[l], 1)

    def dve_norm(self, dve, k, v, l=0, first=False):
        if has(k - 2) and not first:
            if l + 1 == self.levels:
                dve.wait_ge(self.transposed, k - 1)
            else:
                dve.wait_ge(self.normed[l + 1], k - 1)
        dve.wait_ge(self.rstd_made[l], k + 1)
        src = self.g["xs"][:, bass.ds(k, 1), :].rearrange("p a d -> p (a d)") if l == 0 else self.xn[:, v, 0, :]
        dve.tensor_scalar(self.xn[:, v, l, :], src, self.mv[:, v, l, 0:1], self.rstd[:, v, l:l + 1],
                          ALU.subtract, ALU.mult).then_inc(self.normed[l], 1)
        if self.keep:
            dve.wait_ge(self.normed[l], k + 1)
            dve.tensor_tensor(src, src, self.xn[:, v, 0, :], ALU.add).then_inc(self.kept, 1)
        if self.rows:
            dve.tensor_scalar(self.g["xn"][:, bass.ds(k, 1), :].rearrange("p a d -> p (a d)"), src, self.mv[:, v, l, 0:1],
                              self.rstd[:, v, l:l + 1], ALU.subtract, ALU.mult).then_inc(self.kept, 1)

    def pe_transpose(self, pe, k, v, dst):
        pe.wait_ge(self.normed[self.levels - 1], k + 1)
        if has(k - 1):
            pe.wait_ge(self.copied, k)
        pe.transpose(dst, self.xn[:, v, self.levels - 1, :], self.g["ident"][:, :]).then_inc(self.transposed, 1)

    def act_copy(self, act, k, src):
        act.wait_ge(self.transposed, k + 1)
        dst = self.g["xnT"][:, bass.ds(k * P, P)]
        if self.levels == 1:
            act.activation(dst, src, ACT.Copy).then_inc(self.copied, 1)
        else:
            act.activation(dst, src, ACT.Identity, bias=self.g["gbl"][:, 1:2],
                           scale=self.g["gbl"][:, 0:1]).then_inc(self.copied, 1)


NH, HD = 16, 8


def attention(nc, g, io, layer):
    rope = layer == 0
    R = 4
    names = ["wq", "wk", "wv", "wo"] + (["wqs", "wks"] if rope else [])
    with Mem(nc, f"at{layer}") as m:
        w = {n: m.sb(n, [P, P]) for n in names}
        heads = m.sb("heads", [P, NH])
        pick, bias = m.sb("pick", [P, P], BF16), m.sb("bias", [P, NH * S], BF16)
        loads = [(w[n][:, :], io[f"w{layer}_{n}"]) for n in names]
        loads += [(heads[:, :], io["c_heads"]), (pick[:, :], io["c_pick"]), (bias[:, :], io[f"c_bias{layer}"])]
        if rope:
            table = m.sb("table", [P, 4, S])
            cols = m.sb("cols", [P, 5])
            bo = m.sb("bo", [P, D])
            loads += [(table[:, :, :], io["c_rope8"].rearrange("p (a s) -> p a s", a=4)), (cols[:, :], io["w0_cols"]),
                      (bo[:, :], io["w0_bo"].rearrange("(a d) -> a d", a=1).to_broadcast([P, D]))]
            terms = m.sb("terms", [P, 2, 4, P])
        xg = m.sb("xg", [P, R, P])
        qT = m.sb("qT", [P, R, P])
        kT = m.sb("kT", [P, R, P])
        kblk = m.sb("kblk", [P, 2, PER, NH * S])
        vblk = m.sb("vblk", [P, R, PER, NH // 2, 48])
        pr = m.sb("pr", [P, R, NH * S])
        small = m.sb("small", [P, R, 3, NH])
        pT = m.sb("pT", [P, 2, NH // 2, P])
        oT = m.sb("oT", [P, 2, P])
        p_qk, p_v, p_o, p_y = m.ps("p_qk"), m.ps("p_v"), m.ps("p_o"), m.ps("p_y")
        p_s = [m.ps(f"p_s{i}") for i in range(2)]
        p_t = [m.ps(f"p_t{i}") for i in range(2)]
        consts_in, zeroed = m.sem("consts_in"), m.sem("zeroed")
        xg_copied, qk_done, v_done, v_copied = m.sem("xg_copied"), m.sem("qk_done"), m.sem("v_done"), m.sem("v_copied")
        q_terms, k_terms, q_ready, k_ready, kblk_ready = (m.sem(n) for n in ("q_terms", "k_terms", "q_ready", "k_ready", "kblk_ready"))
        s_done, maxed, exped, centred, c_exped = (m.sem(n) for n in ("s_done", "maxed", "exped", "centred", "c_exped"))
        summed, inverted, probs_ready = m.sem("summed"), m.sem("inverted"), m.sem("probs_ready")
        pt_done, pt_copied, pv_done, oT_copied, y_done = (m.sem(n) for n in ("pt_done", "pt_copied", "pv_done", "oT_copied", "y_done"))
        x_part, x_made = m.sem("x_part"), m.sem("x_made")
        levels = 1 if rope else 2
        norm = Norm(m, g, levels, x_made)
        block = m.stack.enter_context(nc.Block())
        first, last = -5, NT + 2 + levels
        half = NH * S // 2
        HH = NH // 2

        @block.sync
        def _(sync):
            for dst, src in loads:
                sync.dma_start(dst, src).then_inc(consts_in, 16)

        @block.tensor
        def _(pe):
            pe.wait_ge(consts_in, 16 * len(loads))
            pe.wait_ge(zeroed, 1)
            wv = w["wv"][:, :].rearrange("i (j h d) -> i h j d", j=NH // 2, h=2)

            def turn(t, u):
                k, v = t - 1, (u - 1) % R
                if has(k):
                    pe.wait_ge(probs_ready, k + 1)
                    for hf in range(2):
                        if has(k - 1):
                            pe.wait_ge(pt_copied, 2 * k + hf - 1)
                        for j in range(4):
                            mm = pe.transpose(p_t[hf][:, j * P:(j + 1) * P],
                                              pr[:, v, hf * half + j * P:hf * half + (j + 1) * P], g["ident"][:, :])
                        mm.then_inc(pt_done, 1)
                k = t - 2
                if has(k):
                    pe.wait_ge(oT_copied, k + 1)
                    if has(k - 1):
                        pe.wait_ge(x_made, k)
                    if has(k - levels - 1):
                        pe.wait_ge(norm.copied, k - levels)
                    pe.matmul(p_y[:, 0:D], oT[:, u % 2, :], w["wo"][:, :], start=True, stop=True).then_inc(y_done, 1)
                k = t + 4
                if has(k):
                    pe.wait_ge(xg_copied, k + 1)
                    if has(k - 1):
                        if rope:
                            pe.wait_ge(k_terms, 2 * k)
                        else:
                            pe.wait_ge(k_ready, k)
                    for i, n in enumerate(["wq", "wqs", "wk", "wks"] if rope else ["wq", "wk"]):
                        mm = pe.matmul(p_qk[:, i * P:(i + 1) * P], w[n][:, :], xg[:, u, :], start=True, stop=True)
                    mm.then_inc(qk_done, 1)
                k, v = t + 2, (u + 2) % R
                if has(k):
                    if has(k - 1):
                        pe.wait_ge(v_copied, 2 * k)
                    for h in range(2):
                        for b in range(PER):
                            mm = pe.matmul(p_v[S * h:S * h + S, b * S:(b + 1) * S], xg[:, v, b * S:(b + 1) * S],
                                           wv[:, h], start=True, stop=True)
                    mm.then_inc(v_done, 1)
                k, v = t - 1, (u - 1) % R
                if has(k):
                    pe.wait_ge(v_copied, 2 * (k + 1))
                    if has(k - 1):
                        pe.wait_ge(oT_copied, k)
                    pe.wait_ge(pt_copied, 2 * k + 2)
                    for c in range(4):
                        for b in range(PER):
                            for par in range(2):
                                j = 2 * c + par
                                at = 16 * (1 - par)
                                mm = pe.matmul(p_o[32 * c:32 * c + 32, b * S:(b + 1) * S], vblk[:, v, b, j, at:at + 32],
                                               pT[:, v % 2, j, b * S:(b + 1) * S], start=par == 0, stop=par == 1)
                    mm.then_inc(pv_done, 1)
                k, v = t - 2 - levels, (u - levels) % 2
                if has(k):
                    if has(t - 2):
                        pe.wait_ge(x_made, t - 1)
                    norm.pe_transpose(pe, k, v, p_y[:, P:2 * P])
                k, v = t + 2, (u + 2) % R
                if has(k):
                    pe.wait_ge(q_ready, k + 1)
                    pe.wait_ge(kblk_ready, k + 1)
                    for hf in range(2):
                        if has(k - 1):
                            pe.wait_ge(centred if hf else exped, k)
                        pe.matmul(p_s[hf][:, :], pick[:, :], bias[:, hf * half:(hf + 1) * half], start=True, stop=False)
                        for b in range(PER):
                            mm = pe.matmul(p_s[hf][S * b:S * b + S, :], qT[:, v, b * S:(b + 1) * S],
                                           kblk[:, v % 2, b, hf * half:(hf + 1) * half], start=False, stop=True)
                        mm.then_inc(s_done, 1)

            turns(pe, turn, first, last, R, head=2, tail=2)

        @block.vector
        def _(dve):
            dve.memset(vblk[:, :, :, :, :], 0.0).then_inc(zeroed, 1)
            dve.wait_ge(consts_in, 16 * len(loads))

            def turn(t, u):
                k, v = t + 1, (u + 1) % R
                if has(k):
                    scores = [p_s[hf][:, :].rearrange("p (h k) -> p h k", h=HH) for hf in range(2)]
                    dve.wait_ge(s_done, 2 * k + 1)
                    dve.tensor_reduce(small[:, v, 0, 0:HH], scores[0], AX, ALU.max, negate=True).then_inc(maxed, 1)
                    dve.wait_ge(s_done, 2 * k + 2)
                    dve.tensor_reduce(small[:, v, 0, HH:NH], scores[1], AX, ALU.max, negate=True).then_inc(maxed, 1)
                    if has(k - R):
                        dve.wait_ge(pt_done, 2 * (k - R + 1))
                    dve.wait_ge(maxed, 2 * k + 2)
                    dve.tensor_tensor(pr[:, v, half:].rearrange("p (h k) -> p h k", h=HH), scores[1],
                                      col_bc(small[:, v, 0, HH:NH], S), ALU.add).then_inc(centred, 1)
                k = t - 2
                if has(k):
                    x = g["xs"][:, bass.ds(k, 1), :].rearrange("p a d -> p (a d)")
                    dve.wait_ge(y_done, k + 1)
                    if rope:
                        dve.tensor_tensor(x, x, bo[:, :], ALU.add).then_inc(x_part, 1)
                        dve.wait_ge(x_part, k + 1)
                    dve.tensor_tensor(x, p_y[:, 0:D], x, ALU.add).then_inc(x_made, 1)
                    norm.dve_stats(dve, k, u % 2)
                if levels == 2 and has(t - 3):
                    norm.dve_stats(dve, t - 3, (u - 1) % 2, 1)
                k, v = t, u
                if has(k):
                    dve.wait_ge(c_exped, k + 1)
                    dve.tensor_reduce(small[:, v, 1, HH:NH], pr[:, v, half:].rearrange("p (h k) -> p h k", h=HH), AX, ALU.add).then_inc(summed, 1)
                k, v = t + 4, u % 2
                if rope and has(k):
                    dve.wait_ge(qk_done, k + 1)
                    if has(k - 2):
                        dve.wait_ge(k_ready, k - 1)
                        dve.wait_ge(q_ready, k - 1)
                    for i in range(4):
                        dve.scalar_tensor_tensor(
                            terms[:, v, i, :].rearrange("p (b s) -> p b s", b=PER),
                            p_qk[:, i * P:(i + 1) * P].rearrange("p (b s) -> p b s", b=PER), cols[:, i:i + 1],
                            row_bc(table[:, i, :], PER), ALU.add, ALU.mult).then_inc(q_terms if i < 2 else k_terms, 1)
                k, v = t, u
                if has(k):
                    dve.wait_ge(summed, k + 1)
                    dve.reciprocal(small[:, v, 2, :], small[:, v, 1, :]).then_inc(inverted, 1)
                if has(t - 2):
                    norm.dve_norm(dve, t - 2, u % 2)
                if levels == 2 and has(t - 3):
                    norm.dve_norm(dve, t - 3, (u - 1) % 2, 1)
                if has(k):
                    dve.wait_ge(inverted, k + 1)
                    dve.tensor_tensor(pr[:, v, :].rearrange("p (h k) -> p h k", h=NH), pr[:, v, :].rearrange("p (h k) -> p h k", h=NH),
                                      col_bc(small[:, v, 2, :], S), ALU.mult).then_inc(probs_ready, 1)

            turns(dve, turn, first, last, R, head=2, tail=2)

        @block.gpsimd
        def _(pool):
            pool.wait_ge(consts_in, 16 * len(loads))

            def turn(t, u):
                k, v = t + 3, (u + 3) % R
                if rope and has(k):
                    pool.wait_ge(q_terms, 2 * (k + 1))
                    if has(k - R):
                        pool.wait_ge(s_done, 2 * (k - R + 1))
                    pool.tensor_tensor(qT[:, v, :], terms[:, v % 2, 0, :], terms[:, v % 2, 1, :], ALU.add).then_inc(q_ready, 1)
                    pool.wait_ge(k_terms, 2 * (k + 1))
                    if has(k - R):
                        pool.wait_ge(kblk_ready, k - R + 1)
                    pool.tensor_tensor(kT[:, v, :], terms[:, v % 2, 2, :], terms[:, v % 2, 3, :], ALU.add).then_inc(k_ready, 1)
                if has(k):
                    pool.wait_ge(k_ready, k + 1)
                    if has(k - 2):
                        pool.wait_ge(s_done, 2 * (k - 1))
                    for b in range(PER):
                        op = pool.tensor_tensor(kblk[:, v % 2, b, :].rearrange("p (h k) -> p h k", h=NH),
                                                row_bc(kT[:, v, b * S:(b + 1) * S], NH), col_bc(heads[:, :], S), ALU.mult)
                    op.then_inc(kblk_ready, 1)
                if has(t - 2):
                    norm.pool_rstd(pool, t - 2, u % 2)
                if levels == 2 and has(t - 3):
                    norm.pool_rstd(pool, t - 3, (u - 1) % 2, 1)

            turns(pool, turn, first, last, R, head=2, tail=2)

        @block.scalar
        def _(act):
            act.wait_ge(consts_in, 16 * len(loads))
            act.wait_ge(zeroed, 1)

            def turn(t, u):
                k, v = t - 1, (u - 1) % 2
                if has(k):
                    for hf in range(2):
                        act.wait_ge(pt_done, 2 * k + hf + 1)
                        if has(k - 2):
                            act.wait_ge(pv_done, k - 1)
                        act.activation(pT[:, v, 4 * hf:4 * hf + 4, :].rearrange("p j q -> p (j q)"), p_t[hf][:, :],
                                       ACT.Copy).then_inc(pt_copied, 1)
                k, v = t + 1, (u + 1) % R
                if has(k):
                    act.wait_ge(maxed, 2 * k + 1)
                    if has(k - R):
                        act.wait_ge(pt_done, 2 * (k - R + 1))
                    for h in range(HH):
                        op = act.activation(pr[:, v, h * S:(h + 1) * S], p_s[0][:, h * S:(h + 1) * S], ACT.Exp,
                                            bias=small[:, v, 0, h:h + 1], accum_out=small[:, v, 1, h:h + 1])
                    op.then_inc(exped, 1)
                    act.wait_ge(centred, k + 1)
                    act.activation(pr[:, v, half:], pr[:, v, half:], ACT.Exp).then_inc(c_exped, 1)
                k, v = t + 4, u
                if not rope and has(k):
                    act.wait_ge(qk_done, k + 1)
                    if has(k - R):
                        act.wait_ge(s_done, 2 * (k - R + 1))
                        act.wait_ge(kblk_ready, k - R + 1)
                    act.activation(qT[:, v, :], p_qk[:, 0:P], ACT.Copy, scale=float(HD) ** -0.5).then_inc(q_ready, 1)
                    act.activation(kT[:, v, :], p_qk[:, P:2 * P], ACT.Copy).then_inc(k_ready, 1)
                k, v = t + 2, (u + 2) % R
                if has(k):
                    act.wait_ge(v_done, k + 1)
                    if has(k - R):
                        act.wait_ge(pv_done, k - R + 1)
                    for h in range(2):
                        rows = slice(S * h, S * h + S)
                        act.activation(vblk[rows, v, :, :, 16 + 8 * h:24 + 8 * h].rearrange("p b j d -> p (b j) d"),
                                       p_v[rows, 0:2 * S].rearrange("p (c d) -> p c d", d=HD), ACT.Copy).then_inc(v_copied, 1)
                k, v = t - 1, (u - 1) % 2
                if has(k):
                    act.wait_ge(pv_done, k + 1)
                    if has(k - 2):
                        act.wait_ge(y_done, k - 1)
                    if rope:
                        act.activation(oT[:, v, :], p_o[:, 0:P], ACT.Identity, bias=cols[:, 4:5]).then_inc(oT_copied, 1)
                    else:
                        act.activation(oT[:, v, :], p_o[:, 0:P], ACT.Copy).then_inc(oT_copied, 1)
                k = t + 5
                if has(k):
                    if has(k - R):
                        act.wait_ge(v_done, k - R + 1)
                    act.activation(xg[:, (u + 1) % R, :], g["xnT"][:, bass.ds(k * P, P)], ACT.Copy).then_inc(xg_copied, 1)
                if has(t - 2 - levels):
                    norm.act_copy(act, t - 2 - levels, p_y[:, P:2 * P])

            turns(act, turn, first, last, R, head=2, tail=2)


MH, MD = 4, 32


def mlstm(nc, g, io, keep=True):
    R = 4
    W = MH * S
    with Mem(nc, "ml") as m:
        wg = m.sb("wg", [P, 3, 2 * MH])
        bg = m.sb("bg", [P, 2 * MH])
        same, tri = m.sb("same", [P, P]), m.sb("tri", [P, P])
        diag, causal = m.sb("diag", [P, S]), m.sb("causal", [P, S])
        scale = m.sb("scale", [P, D])
        loads = [(wg[:, a, :], io["w_mgates"][a * D:(a + 1) * D, :]) for a in range(3)]
        loads += [(bg[:, :], io["w_mbias"].rearrange("(a d) -> a d", a=1).to_broadcast([P, 2 * MH])),
                 (same[:, :], io["c_same"]), (tri[:, :], io["c_tri"]), (diag[:, :], io["c_diag"]), (causal[:, :], io["c_causal"]),
                 (scale[:, :], io["w_mscale"].rearrange("(a d) -> a d", a=1).to_broadcast([P, D]))]
        vals = m.sb("vals", [P, NT, PER, MH // 2, MD])
        v_d = io["ctx_1024"].rearrange("(t b) s (j h d) -> b j h s t d", b=PER, j=MH // 2, h=2)
        for h in range(2):
            for b in range(PER):
                for j in range(MH // 2):
                    loads.append((vals[S * h:S * h + S, :, b, j, :], v_d[b, j, h]))
        gates = m.sb("gates", [P, NT, 2 * MH])
        nabs, expn, logf = m.sb("nabs", [P, NT, MH]), m.sb("expn", [P, NT, MH]), m.sb("logf", [P, NT, MH])
        cs, uu = m.sb("cs", [P, NT, MH]), m.sb("uu", [P, NT, MH])
        xg = m.sb("xg", [P, 2, P])
        rdiag = m.sb("rdiag", [P, 2, MH, S])
        kblk = m.sb("kblk", [P, 2, PER, MH, S])
        vblk = m.sb("vblk", [P, 2, PER, MH // 2, 2, MD])
        dd = m.sb("dd", [P, 2, MH, S])
        cc = m.sb("cc", [P, 2, MH, S])
        pT = m.sb("pT", [P, 2, 2, P])
        sm = m.sb("sm", [P, 2, 6, MH])
        hst, hmv, hrs = m.sb("hst", [P, 2, MH, 6]), m.sb("hmv", [P, 2, MH, 2]), m.sb("hrs", [P, 2, MH])
        hh = m.sb("hh", [P, 2, MH, MD])
        p_x = [m.ps(f"p_x{i}") for i in range(2)]
        p_h = [m.ps(f"p_h{i}") for i in range(2)]
        p_g, p_t, p_n = m.ps("p_g"), m.ps("p_t"), m.ps("p_n")
        consts_in, zeroed = m.sem("consts_in"), m.sem("zeroed")
        gates_done, gate_step, logs, cs_done, u_made = (m.sem(n) for n in ("gates_done", "gate_step", "logs", "cs_done", "u_made"))
        xg_copied, r_ready, kblk_ready, vblk_ready = (m.sem(n) for n in ("xg_copied", "r_ready", "kblk_ready", "vblk_ready"))
        x_done, d_step, exped, c_step, inverted, c_ready = (
            m.sem(n) for n in ("x_done", "d_step", "exped", "c_step", "inverted", "c_ready"))
        pt_done, pt_copied, pv_done = m.sem("pt_done"), m.sem("pt_copied"), m.sem("pv_done")
        h_stats, h_moments, h_var, h_rstd, h_step, x_made = (m.sem(n) for n in ("h_stats", "h_moments", "h_var", "h_rstd", "h_step", "x_made"))
        norm = Norm(m, g, 1, x_made, keep)
        block = m.stack.enter_context(nc.Block())
        first, last = -2, NT + 3
        D_STEPS, C_STEPS, H_STEPS = 4, 5, 3

        @block.sync
        def _(sync):
            for dst, src in loads:
                sync.dma_start(dst, src).then_inc(consts_in, 16)

        @block.tensor
        def _(pe):
            pe.wait_ge(consts_in, 16 * len(loads))
            for t in range(NT):
                cols = slice(t * 2 * MH, (t + 1) * 2 * MH)
                pe.matmul(p_g[:, cols], g["xnT"][:, t * P:(t + 1) * P], wg[:, 0, :], start=True, stop=False)
                pe.matmul(p_g[:, cols], g["ctxT"][:, t * P:(t + 1) * P], wg[:, 1, :], start=False, stop=False)
                mm = pe.matmul(p_g[:, cols], g["ctxT"][:, t * P:(t + 1) * P], wg[:, 2, :], start=False, stop=True)
            mm.then_inc(gates_done, 1)
            pe.wait_ge(gate_step, 3)
            pe.matmul(p_t[:, 0:NT * MH], tri[:, :], logf[:, :, :].rearrange("p t h -> p (t h)"), start=True, stop=True).then_inc(cs_done, 1)

            def turn(t, u):
                k, v = t + 1, (u + 1) % 2
                if has(k):
                    pe.wait_ge(r_ready, k + 1)
                    if has(k - 2):
                        pe.wait_ge(c_step, C_STEPS * (k - 2) + 1)
                    pe.matmul(p_x[v][:, 0:W], same[:, :], rdiag[:, v, :, :].rearrange("p h k -> p (h k)"), start=True, stop=True)
                    pe.wait_ge(kblk_ready, MH * (k + 1))
                    pe.wait_ge(xg_copied, k + 1)
                    for b in range(PER):
                        mm = pe.matmul(p_x[v][S * b:S * b + S, W:2 * W], xg[:, v, b * S:(b + 1) * S],
                                       kblk[:, v, b, :, :].rearrange("p h k -> p (h k)"), start=True, stop=True)
                    mm.then_inc(x_done, 1)
                if has(t):
                    pe.wait_ge(c_ready, t + 1)
                    if has(t - 1):
                        pe.wait_ge(pt_copied, t)
                    else:
                        pe.wait_ge(u_made, 2)
                    for j in range(2):
                        mm = pe.transpose(p_t[:, j * P:(j + 1) * P],
                                          cc[:, u % 2, 2 * j:2 * j + 2, :].rearrange("p h k -> p (h k)"), g["ident"][:, :])
                    mm.then_inc(pt_done, 1)
                    pe.wait_ge(vblk_ready, 2 * (t + 1))
                    if has(t - 2):
                        pe.wait_ge(h_step, H_STEPS * (t - 2) + 1)
                    pe.wait_ge(pt_copied, t + 1)
                    for b in range(PER):
                        for j in range(2):
                            mm = pe.matmul(p_h[u % 2][S * b:S * b + S, j * 2 * MD:(j + 1) * 2 * MD], pT[:, u % 2, j, b * S:(b + 1) * S],
                                           vblk[:, u % 2, b, j, :, :].rearrange("p h d -> p (h d)"), start=True, stop=True)
                    mm.then_inc(pv_done, 1)
                if has(t - 2):
                    norm.pe_transpose(pe, t - 2, u % 2, p_n[:, 0:P])

            turns(pe, turn, first, last, R)

        @block.vector
        def _(dve):
            dve.memset(kblk[:, :, :, :, :], 0.0).then_inc(zeroed, 1)
            dve.memset(vblk[:, :, :, :, :, :], 0.0).then_inc(zeroed, 1)
            dve.wait_ge(consts_in, 16 * len(loads))
            dve.wait_ge(gates_done, 1)
            dve.tensor_tensor(gates[:, :, :], p_g[:, 0:NT * 2 * MH].rearrange("p (t n) -> p t n", t=NT), row_bc(bg[:, :], NT),
                              ALU.add).then_inc(gate_step, 1)
            dve.wait_ge(gate_step, 1)
            ig, fg = gates[:, :, 0:MH], gates[:, :, MH:2 * MH]
            dve.scalar_tensor_tensor(nabs[:, :, :], fg, -1.0, fg, ALU.mult, ALU.min).then_inc(gate_step, 1)
            dve.wait_ge(logs, 2)
            dve.scalar_tensor_tensor(logf[:, :, :], fg, 0.0, expn[:, :, :], ALU.min, ALU.subtract).then_inc(gate_step, 1)
            dve.wait_ge(cs_done, 1)
            cs_p = p_t[:, 0:NT * MH].rearrange("p (t h) -> p t h", t=NT)
            dve.tensor_copy(cs[:, :, :], cs_p).then_inc(u_made, 1)
            dve.tensor_tensor(uu[:, :, :], ig, cs_p, ALU.subtract).then_inc(u_made, 1)
            dve.wait_ge(u_made, 2)

            def turn(t, u):
                k, v = t + 1, (u + 1) % 2
                mx, mm, en, sc, nm, inv = (sm[:, v, i, :] for i in range(6))
                U = p_x[v][:, 0:W].rearrange("p (h k) -> p h k", h=MH)
                QK = p_x[v][:, W:2 * W].rearrange("p (h k) -> p h k", h=MH)
                if has(k):
                    dve.wait_ge(x_done, k + 1)
                    if has(k - 2):
                        dve.wait_ge(c_step, C_STEPS * (k - 2) + 1)
                    dve.tensor_tensor(dd[:, v], U, row_bc(causal[:, :], MH), ALU.add).then_inc(d_step, 1)
                    dve.wait_ge(d_step, D_STEPS * k + 1)
                    dve.tensor_reduce(mx, dd[:, v], AX, ALU.max).then_inc(d_step, 1)
                    dve.wait_ge(d_step, D_STEPS * k + 2)
                    dve.tensor_tensor(dd[:, v], dd[:, v], col_bc(mx, S), ALU.subtract).then_inc(d_step, 1)
                    dve.tensor_tensor(mm, cs[:, bass.ds(k, 1), :].rearrange("p a h -> p (a h)"), mx, ALU.add).then_inc(d_step, 1)
                n, w = t - 1, (u - 1) % 2
                if has(n):
                    H = p_h[w][:, 0:D].rearrange("p (h d) -> p h d", h=MH)
                    dve.wait_ge(h_rstd, n + 1)
                    if has(n - 2):
                        dve.wait_ge(x_made, n - 1)
                    dve.tensor_tensor(hh[:, w], H, hmv[:, w, :, 0:1].to_broadcast([P, MH, MD]), ALU.subtract).then_inc(h_step, 1)
                    dve.wait_ge(h_step, H_STEPS * n + 1)
                    dve.tensor_tensor(hh[:, w], hh[:, w], col_bc(hrs[:, w, :], MD), ALU.mult).then_inc(h_step, 1)
                    dve.wait_ge(h_step, H_STEPS * n + 2)
                    hf = hh[:, w].rearrange("p h d -> p (h d)")
                    dve.tensor_tensor(hf, hf, scale[:, :], ALU.mult).then_inc(h_step, 1)
                    dve.wait_ge(h_step, H_STEPS * n + 3)
                    x = g["xs"][:, bass.ds(n, 1), :].rearrange("p a d -> p (a d)")
                    dve.tensor_tensor(x, x, hf, ALU.add).then_inc(x_made, 1)
                    norm.dve_stats(dve, n, w)
                if has(k):
                    dve.wait_ge(exped, 2 * (k + 1))
                    if has(k - 2):
                        dve.wait_ge(pt_done, k - 1)
                    dve.tensor_tensor(cc[:, v], QK, dd[:, v], ALU.mult).then_inc(c_step, 1)
                    dve.wait_ge(c_step, C_STEPS * k + 1)
                    dve.tensor_reduce(sc, cc[:, v], AX, ALU.add).then_inc(c_step, 1)
                    dve.wait_ge(c_step, C_STEPS * k + 2)
                    dve.scalar_tensor_tensor(nm, sc, -1.0, sc, ALU.mult, ALU.max).then_inc(c_step, 1)
                    dve.wait_ge(c_step, C_STEPS * k + 3)
                    dve.scalar_tensor_tensor(nm, nm, 1.0, en, ALU.mult, ALU.max).then_inc(c_step, 1)
                    dve.wait_ge(c_step, C_STEPS * k + 4)
                    dve.tensor_scalar(nm, nm, 1e-6, None, ALU.add).then_inc(c_step, 1)
                    dve.wait_ge(c_step, C_STEPS * k + 5)
                    dve.reciprocal(inv, nm).then_inc(inverted, 1)
                    dve.wait_ge(inverted, k + 1)
                    dve.tensor_tensor(cc[:, v], cc[:, v], col_bc(inv, S), ALU.mult).then_inc(c_ready, 1)
                if has(t - 2):
                    norm.dve_norm(dve, t - 2, u % 2)
                if has(t):
                    dve.wait_ge(pv_done, t + 1)
                    if has(t - 2):
                        dve.wait_ge(h_rstd, t - 1)
                    carry(dve, g)
                    for h in range(MH):
                        dve.bn_stats(hst[:, u % 2, h, :], p_h[u % 2][:, h * MD:(h + 1) * MD]).then_inc(h_stats, 1)
                    if has(t - 2):
                        dve.wait_ge(h_step, H_STEPS * (t - 2) + 1)
                    dve.wait_ge(h_stats, MH * (t + 1))
                    carry(dve, g)
                    for h in range(MH):
                        dve.bn_aggr(hmv[:, u % 2, h, :], hst[:, u % 2, h, :]).then_inc(h_moments, 1)

            turns(dve, turn, first, last, R)

        @block.gpsimd
        def _(pool):
            pool.wait_ge(consts_in, 16 * len(loads))
            pool.wait_ge(u_made, 2)

            def turn(t, u):
                k = t + 2
                if has(k):
                    if has(k - 2):
                        pool.wait_ge(x_done, k - 1)
                    pool.tensor_tensor(rdiag[:, u % 2], row_bc(diag[:, :], MH),
                                       col_bc(uu[:, bass.ds(k, 1), :].rearrange("p a h -> p (a h)"), S), ALU.mult).then_inc(r_ready, 1)
                if has(t - 1):
                    norm.pool_rstd(pool, t - 1, (u - 1) % 2)
                if has(t):
                    pool.wait_ge(h_moments, MH * (t + 1))
                    if has(t - 2):
                        pool.wait_ge(h_step, H_STEPS * (t - 2) + 2)
                    rs = hrs[:, u % 2, :]
                    pool.tensor_tensor(rs, hmv[:, u % 2, :, 1], g["eps"][:, :], ALU.add).then_inc(h_var, 1)
                    pool.wait_ge(h_var, t + 1)
                    pool.tensor_tensor(rs, rs, g["neghalf"][:, :], ALU.pow).then_inc(h_rstd, 1)

            turns(pool, turn, first, last, R)

        @block.scalar
        def _(act):
            act.wait_ge(consts_in, 16 * len(loads))
            act.wait_ge(zeroed, 2)
            act.wait_ge(gate_step, 2)
            act.activation(nabs[:, :, :], nabs[:, :, :], ACT.Exp).then_inc(logs, 1)
            act.wait_ge(logs, 1)
            act.activation(expn[:, :, :], nabs[:, :, :], ACT.Ln, bias=1.0).then_inc(logs, 1)

            def turn(t, u):
                k, v = t + 2, u % 2
                if has(k):
                    if has(k - 2):
                        act.wait_ge(x_done, k - 1)
                    act.activation(xg[:, v, :], g["xnT"][:, bass.ds(k * P, P)], ACT.Copy).then_inc(xg_copied, 1)
                    for h in range(MH):
                        rows = slice(MD * h, MD * h + MD)
                        act.activation(kblk[rows, v, :, h, :], g["ctxT"][rows, bass.ds(k * P, P)].rearrange("p (b k) -> p b k", b=PER),
                                       ACT.Copy, scale=float(MD) ** -0.5).then_inc(kblk_ready, 1)
                k, v = t + 1, (u + 1) % 2
                if has(k):
                    if has(k - 2):
                        act.wait_ge(pv_done, k - 1)
                    for h in range(2):
                        rows = slice(S * h, S * h + S)
                        act.activation(vblk[rows, v, :, :, h, :].rearrange("p b j d -> p (b j) d"),
                                       vals[rows, bass.ds(k, 1), :, :, :].rearrange("p a b j d -> p (a b j) d"), ACT.Copy).then_inc(vblk_ready, 1)
                    act.wait_ge(d_step, D_STEPS * (k + 1))
                    act.activation(dd[:, v], dd[:, v], ACT.Exp).then_inc(exped, 1)
                    act.activation(sm[:, v, 2, :], sm[:, v, 1, :], ACT.Exp, scale=-1.0).then_inc(exped, 1)
                if has(t):
                    act.wait_ge(pt_done, t + 1)
                    if has(t - 2):
                        act.wait_ge(pv_done, t - 1)
                    act.activation(pT[:, u % 2].rearrange("p j q -> p (j q)"), p_t[:, 0:2 * P], ACT.Copy).then_inc(pt_copied, 1)
                if has(t - 2):
                    norm.act_copy(act, t - 2, p_n[:, 0:P])

            turns(act, turn, first, last, R)


NE, TOPK = 15, 3
FF, FF_R = 512, 256
CS, CE = FF // P, FF_R // P
NC_FF = CS + NE * CE
NGR = NT // 4


def experts(nc, g, io):
    R = 2
    HR = 4
    N = 512
    with Mem(nc, "ff") as m:
        w1, w2 = m.sb("w1", [P, NC_FF, P]), m.sb("w2", [P, NC_FF, D])
        b1, b2 = m.sb("b1", [P, NC_FF]), m.sb("b2", [NE + 1, D])
        gw, gb = m.sb("gw", [P, NE]), m.sb("gb", [NE, 1])
        spread = m.sb("spread", [P, NE, P], BF16)
        identb = m.sb("identb", [P, P], BF16)
        seg = m.sb("seg", [P, 4 * NE])
        loads = [(gw[:, :], io["L0_ffn_gW"]), (gb[:, :], io["L0_ffn_gb"].rearrange("(e a) -> e a", a=1)),
                 (spread[:, :, :], io["c_spread"].rearrange("p (e m) -> p e m", e=NE)), (identb[:, :], io["c_identb"]),
                 (seg[:, :], io["c_seg"]), (b1[:, :], io["w_b1"]), (b2[:, :], io["w_b2"]),
                 (w1[:, 0:CS, :], io["L0_ffn_sW1"][0].rearrange("i (c f) -> i c f", c=CS)),
                 (w2[:, 0:CS, :], io["L0_ffn_sW2"][0].rearrange("(c f) d -> f c d", c=CS))]
        for e in range(NE):
            at = slice(CS + CE * e, CS + CE * (e + 1))
            loads.append((w1[:, at, :], io["L0_ffn_rW1"][e].rearrange("i (c f) -> i c f", c=CE)))
            loads.append((w2[:, at, :], io["L0_ffn_rW2"][e].rearrange("(c f) d -> f c d", c=CE)))
        hid = m.sb("hid", [P, HR, N])
        yT = m.sb("yT", [P, N])
        lgT = m.sb("lgT", [P, N])
        wt, tmp, eq, cum, sel = (m.sb(n, [P, 4, NE]) for n in ("wt", "tmp", "eq", "cum", "sel"))
        v8 = m.sb("v8", [P, 4, 8])
        s4 = m.sb("s4", [P, 5, 4])
        parts = m.sb("parts", [P, 4, P], BF16)
        partsT = m.sb("partsT", [P, R, N], BF16)
        gT = m.sb("gT", [NE + 1, R, N])
        p_h = [m.ps(f"p_h{i}") for i in range(2)]
        p_b = [m.ps(f"p_b{i}") for i in range(2)]
        p_y, p_t, p_n, p_q = m.ps("p_y"), m.ps("p_t"), m.ps("p_n"), m.ps("p_q")
        consts_in, zeroed = m.sem("consts_in"), m.sem("zeroed")
        w1_done, gelud, scaled, h_used, b_done = (m.sem(n) for n in ("w1_done", "gelud", "scaled", "h_used", "b_done"))
        y_done, y_copied, yt_done, x_made = (m.sem(n) for n in ("y_done", "y_copied", "yt_done", "x_made"))
        q_done, q_copied, lg_done, r_step, r_exped, parts_ready = (
            m.sem(n) for n in ("q_done", "q_copied", "lg_done", "r_step", "r_exped", "parts_ready"))
        pT_done, pT_copied, gT_done, gT_copied = (m.sem(n) for n in ("pT_done", "pT_copied", "gT_done", "gT_copied"))
        norm = Norm(m, g, 1, x_made)
        block = m.stack.enter_context(nc.Block())
        first, last = -1, NGR + 1
        STEPS = 22

        def live(k):
            return has(k, NGR)

        @block.sync
        def _(sync):
            for dst, src in loads:
                sync.dma_start(dst, src).then_inc(consts_in, 16)

        AT_LOGITS, AT_LOGITS_T, AT_PARTS_T, AT_G_T = 1, 3, 26, 30
        AT_YT, AT_STATS, AT_NORM, AT_LNT = 3, (5, 6, 8, 10), (7, 9, 11, 12), (9, 11, 13, 15)

        @block.tensor
        def _(pe):
            pe.wait_ge(consts_in, 16 * len(loads))
            pe.wait_ge(zeroed, 3)

            def turn(t, u):
                on, nxt, old = live(t), live(t + 1), live(t - 1)

                def second(c):
                    if c < CS:
                        pe.wait_ge(gelud, NC_FF * t + c + 1)
                    else:
                        pe.wait_ge(scaled, (NC_FF - CS) * t + c - CS + 1)
                    pe.matmul(p_y[:, :], w2[:, c, :], hid[:, c % HR, :], start=c == 0, stop=False).then_inc(h_used, 1)

                for c in range(NC_FF):
                    if on:
                        if c >= CS and (c - CS) % CE == 0:
                            e = (c - CS) // CE
                            if e == 0:
                                pe.wait_ge(pT_copied, t + 1)
                            if e >= 2:
                                pe.wait_ge(scaled, (NC_FF - CS) * t + CE * (e - 1))
                            elif live(t - 1):
                                pe.wait_ge(scaled, (NC_FF - CS) * t)
                            pe.matmul(p_b[e % 2][:, :], spread[:, e, :], partsT[:, u, :], start=True, stop=True).then_inc(b_done, 1)
                        if c >= 2:
                            pe.wait_ge(gelud, NC_FF * t + c - 1)
                        elif live(t - 1):
                            pe.wait_ge(gelud, NC_FF * t)
                        pe.matmul(p_h[c % 2][:, :], w1[:, c, :], g["xnT"][:, bass.ds(t * N, N)], start=True, stop=True).then_inc(w1_done, 1)
                        if c == 2 and live(t - 1):
                            pe.wait_ge(y_copied, t)
                        if c >= 2:
                            second(c - 2)
                    if c == AT_LOGITS and nxt:
                        if live(t):
                            pe.wait_ge(gT_copied, t + 1)
                        pe.matmul(p_q[0:NE, :], gw[:, :], g["xnT"][:, bass.ds((t + 1) * N, N)], start=True, stop=True).then_inc(q_done, 1)
                    if c == AT_LOGITS_T and nxt:
                        pe.wait_ge(q_copied, t + 2)
                        for q in range(4):
                            mm = pe.transpose(p_q[:, q * P:(q + 1) * P], lgT[:, q * P:(q + 1) * P], g["ident"][:, :])
                        mm.then_inc(lg_done, 1)
                    if c == AT_PARTS_T and nxt:
                        pe.wait_ge(parts_ready, t + 2)
                        for q in range(4):
                            mm = pe.transpose(p_q[:, :].bitcast(BF16)[:, q * P:(q + 1) * P], parts[:, q, :], identb[:, :])
                        mm.then_inc(pT_done, 1)
                    if c == AT_G_T and nxt:
                        pe.wait_ge(pT_copied, t + 2)
                        for q in range(4):
                            mm = pe.transpose(p_q[0:NE, q * P:(q + 1) * P], sel[:, q, :], g["ident"][:, :])
                        mm.then_inc(gT_done, 1)
                    if c == AT_YT and old:
                        pe.wait_ge(y_copied, t)
                        if live(t - 2):
                            pe.wait_ge(x_made, 4 * (t - 1))
                        for q in range(4):
                            mm = pe.transpose(p_t[:, q * P:(q + 1) * P], yT[:, q * P:(q + 1) * P], g["ident"][:, :])
                        mm.then_inc(yt_done, 1)
                    if c in AT_LNT and old:
                        q = AT_LNT.index(c)
                        k = 4 * (t - 1) + q
                        pe.wait_ge(norm.normed[0], k + 1)
                        if q > 0 or live(t - 2):
                            pe.wait_ge(norm.copied, k)
                        pe.transpose(p_n[:, 0:P], norm.xn[:, q % 2, 0, :], g["ident"][:, :]).then_inc(norm.transposed, 1)
                if on:
                    for c in range(NC_FF - 2, NC_FF):
                        second(c)
                    pe.wait_ge(gT_copied, t + 1)
                    pe.matmul(p_y[:, :], b2[:, :], gT[:, u, :], start=False, stop=True).then_inc(y_done, 1)

            turns(pe, turn, first, last, R, NGR)

        @block.vector
        def _(dve):
            dve.memset(lgT[:, :], 0.0).then_inc(zeroed, 1)
            dve.memset(parts[:, :, :], 0.0).then_inc(zeroed, 1)
            dve.memset(gT[:, :, :], 1.0).then_inc(zeroed, 1)
            dve.wait_ge(consts_in, 16 * len(loads))
            dve.wait_ge(zeroed, 3)

            def turn(t, u):
                on, nxt, old = live(t), live(t + 1), live(t - 1)
                lg = p_q[:, :].rearrange("p (q e) -> p q e", q=4)[:, :, 0:NE]
                mx, sm, inv, ngt, room = (s4[:, i, :] for i in range(5))
                kth = v8[:, :, TOPK - 1:TOPK].to_broadcast([P, 4, NE])

                def step(n):
                    dve.wait_ge(r_step, STEPS * (t + 1) + n)

                router = [
                    lambda: (dve.wait_ge(lg_done, t + 2), dve.tensor_reduce(mx, lg, AX, ALU.max).then_inc(r_step, 1)),
                    lambda: (step(1), dve.tensor_tensor(wt[:, :, :], lg, col_bc(mx, NE), ALU.subtract).then_inc(r_step, 1)),
                    lambda: (dve.wait_ge(r_exped, t + 2), dve.tensor_reduce(sm, wt[:, :, :], AX, ALU.add).then_inc(r_step, 1)),
                    lambda: (step(3), dve.reciprocal(inv, sm).then_inc(r_step, 1)),
                    lambda: (step(4), dve.tensor_tensor(wt[:, :, :], wt[:, :, :], col_bc(inv, NE), ALU.mult).then_inc(r_step, 1)),
                    lambda: (step(5), carry(dve, g), [dve.max(v8[:, q, :], wt[:, q, :]).then_inc(r_step, 1) for q in range(4)]),
                    lambda: (step(9), dve.tensor_tensor(tmp[:, :, :], wt[:, :, :], kth, ALU.is_gt).then_inc(r_step, 1)),
                    lambda: dve.tensor_tensor(eq[:, :, :], wt[:, :, :], kth, ALU.is_equal).then_inc(r_step, 1),
                    lambda: (step(10), dve.tensor_reduce(ngt, tmp[:, :, :], AX, ALU.add).then_inc(r_step, 1)),
                    lambda: (step(12), dve.tensor_scalar(room, ngt, -1.0, float(TOPK), ALU.mult, ALU.add).then_inc(r_step, 1)),
                    lambda: (step(11), dve.tensor_tensor_scan(cum[:, :, :].rearrange("p q e -> p (q e)"), seg[:, :],
                                                              eq[:, :, :].rearrange("p q e -> p (q e)"), 0.0, ALU.mult, ALU.add).then_inc(r_step, 1)),
                    lambda: (step(14), dve.tensor_tensor(cum[:, :, :], cum[:, :, :], col_bc(room, NE), ALU.is_le).then_inc(r_step, 1)),
                    lambda: (step(15), dve.tensor_tensor(cum[:, :, :], cum[:, :, :], eq[:, :, :], ALU.mult).then_inc(r_step, 1)),
                    lambda: (step(16), dve.tensor_tensor(cum[:, :, :], cum[:, :, :], tmp[:, :, :], ALU.add).then_inc(r_step, 1)),
                    lambda: (step(17), dve.tensor_tensor(sel[:, :, :], wt[:, :, :], cum[:, :, :], ALU.mult).then_inc(r_step, 1)),
                    lambda: (step(18), dve.tensor_copy(parts[:, :, 0:NE], sel[:, :, :]).then_inc(r_step, 1)),
                    lambda: (step(19), dve.tensor_tensor(tmp[:, :, :], sel[:, :, :], parts[:, :, 0:NE], ALU.subtract).then_inc(r_step, 1)),
                    lambda: (step(20), dve.tensor_copy(parts[:, :, NE:2 * NE], tmp[:, :, :]).then_inc(r_step, 1)),
                    lambda: (step(21), dve.tensor_tensor(tmp[:, :, :], tmp[:, :, :], parts[:, :, NE:2 * NE], ALU.subtract).then_inc(r_step, 1)),
                    lambda: (step(22), dve.tensor_copy(parts[:, :, 2 * NE:3 * NE], tmp[:, :, :]).then_inc(parts_ready, 1)),
                ]
                for c in range(NC_FF):
                    if on and c >= CS:
                        e = (c - CS) // CE
                        dve.wait_ge(gelud, NC_FF * t + c + 1)
                        dve.wait_ge(b_done, NE * t + e + 1)
                        h = hid[:, c % HR, :]
                        dve.tensor_tensor(h, p_b[e % 2][:, :], h, ALU.mult).then_inc(scaled, 1)
                    if c in AT_STATS and old:
                        q = AT_STATS.index(c)
                        k = 4 * (t - 1) + q
                        dve.wait_ge(yt_done, t)
                        x = g["xs"][:, bass.ds(k, 1), :].rearrange("p a d -> p (a d)")
                        dve.tensor_tensor(x, p_t[:, q * P:(q + 1) * P], x, ALU.add).then_inc(x_made, 1)
                        norm.dve_stats(dve, k, q % 2, first=q < 2 and not live(t - 2))
                    if c in AT_NORM and old:
                        q = AT_NORM.index(c)
                        norm.dve_norm(dve, 4 * (t - 1) + q, q % 2, first=q < 2 and not live(t - 2))
                    if nxt and c >= 5 and c - 5 < len(router):
                        router[c - 5]()

            turns(dve, turn, first, last, R, NGR)

        @block.gpsimd
        def _(pool):
            def turn(t, u):
                if live(t - 1):
                    for q in range(4):
                        norm.pool_rstd(pool, 4 * (t - 1) + q, q % 2, first=q < 2 and not live(t - 2))

            turns(pool, turn, first, last, R, NGR)

        @block.scalar
        def _(act):
            act.wait_ge(consts_in, 16 * len(loads))
            act.wait_ge(zeroed, 3)

            def turn(t, u):
                on, nxt, old = live(t), live(t + 1), live(t - 1)
                for c in range(NC_FF):
                    if c == 0 and old:
                        act.wait_ge(y_done, t)
                        if live(t - 2):
                            act.wait_ge(yt_done, t - 1)
                        act.activation(yT[:, :], p_y[:, :], ACT.Copy).then_inc(y_copied, 1)
                    if on:
                        act.wait_ge(w1_done, NC_FF * t + c + 1)
                        if c >= HR:
                            act.wait_ge(h_used, NC_FF * t + c - HR + 1)
                        elif live(t - 1):
                            act.wait_ge(h_used, NC_FF * t)
                        act.activation(hid[:, c % HR, :], p_h[c % 2][:, :], ACT.Gelu, bias=b1[:, c:c + 1]).then_inc(gelud, 1)
                    if c == AT_LOGITS + 1 and nxt:
                        act.wait_ge(q_done, t + 2)
                        act.activation(lgT[0:NE, :], p_q[0:NE, :], ACT.Identity, bias=gb[:, 0:1]).then_inc(q_copied, 1)
                    if c == 7 and nxt:
                        act.wait_ge(r_step, STEPS * (t + 1) + 2)
                        act.activation(wt[:, :, :], wt[:, :, :], ACT.Exp).then_inc(r_exped, 1)
                    if c == AT_PARTS_T + 1 and nxt:
                        act.wait_ge(pT_done, t + 2)
                        act.activation(partsT[:, (u + 1) % 2, :], p_q[:, :].bitcast(BF16)[:, 0:N], ACT.Copy).then_inc(pT_copied, 1)
                    if c == AT_G_T + 1 and nxt:
                        act.wait_ge(gT_done, t + 2)
                        act.activation(gT[0:NE, (u + 1) % 2, :], p_q[0:NE, :], ACT.Copy).then_inc(gT_copied, 1)
                    if c in AT_LNT and old:
                        norm.act_copy(act, 4 * (t - 1) + AT_LNT.index(c), p_n[:, 0:P])

            turns(act, turn, first, last, R, NGR)


XH, XD = 8, 64
XU = XH // 2


def cross_attention(nc, g, io):
    R = 4
    K = 2 * S
    with Mem(nc, "xa") as m:
        wq, wk, wks, wv = (m.sb(n, [P, XH * XD]) for n in ("wq", "wk", "wks", "wv"))
        wo = m.sb("wo", [P, XU, D])
        table = m.sb("table", [P, 2, S])
        loads = [(wq[:, :], io["L1_xattn_Wq"]), (wk[:, :], io["w_xk"]), (wks[:, :], io["w_xks"]), (wv[:, :], io["w_xv"]),
                 (wo[:, :, :], io["L1_xattn_Wo"].rearrange("(u p) d -> p u d", p=P)),
                 (table[:, :, :], io["c_rope64"].rearrange("p (a s) -> p a s", a=2))]
        z = m.sb("z", [P, 2, PER, 2, S])
        qblk = m.sb("qblk", [P, 2, XU, PER, 2, S])
        kT = m.sb("kT", [P, 2, XU, PER, 2, S])
        ksin = m.sb("ksin", [P, XU * PER, S])
        vv = m.sb("vv", [P, 4, PER, XH * XD])
        pr = m.sb("pr", [P, 2, PER, XU, K])
        sm = m.sb("sm", [P, 2, PER, 3, XU])
        pT = m.sb("pT", [P, 2, PER, XU, K])
        oT = m.sb("oT", [P, 2, XU, P])
        pj = [m.ps(f"pj{i}") for i in range(3)]
        p_s = [m.ps(f"p_s{i}") for i in range(2)]
        p_t, p_o, p_y = m.ps("p_t"), m.ps("p_o"), m.ps("p_y")
        consts_in, zeroed = m.sem("consts_in"), m.sem("zeroed")
        z_ready = m.sem("z_ready")
        q_done, k_done, ks_done, v_done = (m.sem(n) for n in ("q_done", "k_done", "ks_done", "v_done"))
        q_ready, k_cos, k_lat, k_sin, k_ready, v_ready = (m.sem(n) for n in ("q_ready", "k_cos", "k_lat", "k_sin", "k_ready", "v_ready"))
        s_done, maxed, exped, inverted, probs_ready = (m.sem(n) for n in ("s_done", "maxed", "exped", "inverted", "probs_ready"))
        pt_done, pt_copied, pv_done, oT_copied, y_done, x_made = (
            m.sem(n) for n in ("pt_done", "pt_copied", "pv_done", "oT_copied", "y_done", "x_made"))
        norm = Norm(m, g, 1, x_made)
        block = m.stack.enter_context(nc.Block())
        first, last = -3, NT + 2

        @block.sync
        def _(sync):
            for dst, src in loads:
                sync.dma_start(dst, src).then_inc(consts_in, 16)

        @block.tensor
        def _(pe):
            pe.wait_ge(consts_in, 16 * len(loads))
            pe.wait_ge(zeroed, 1)

            def scores(k, v, b):
                pe.wait_ge(q_ready, 2 * (k + 1))
                pe.wait_ge(k_lat, 2 * (k + 1))
                pe.wait_ge(k_ready, k + 1)
                if has(k - 1):
                    pe.wait_ge(exped, XH * k - (XU if b == 0 else 0))
                for i in range(XU):
                    mm = pe.matmul(p_s[b][:, i * K:(i + 1) * K], qblk[:, v, i, b, :, :].rearrange("p h q -> p (h q)"),
                                   kT[:, v, i, b, :, :].rearrange("p c k -> p (c k)"), start=True, stop=True)
                mm.then_inc(s_done, 1)

            def turn(t, u):
                k, v = t + 2, u % 2
                if has(k):
                    zall = z[:, v, :, :, :].rearrange("p b c k -> p (b c k)")
                    pe.wait_ge(z_ready, 2 * (k + 1))
                    if has(k - 1):
                        pe.wait_ge(k_sin, k)
                    for i in range(XU):
                        mm = pe.matmul(pj[0][:, i * P:(i + 1) * P], wq[:, i * P:(i + 1) * P], z[:, v, :, 1, :], start=True, stop=True)
                    mm.then_inc(q_done, 1)
                    for i in range(XU):
                        if i % 2 == 0 and has(k - 1):
                            pe.wait_ge(v_ready, PER * k - 1 + i // 2)
                        mm = pe.matmul(pj[1 + i // 2][:, (i % 2) * 2 * P:(i % 2 + 1) * 2 * P], wk[:, i * P:(i + 1) * P], zall,
                                       start=True, stop=True)
                        if i % 2 == 1:
                            mm.then_inc(k_done, 1)
                    pe.wait_ge(q_ready, 2 * (k + 1))
                    for i in range(XU):
                        mm = pe.matmul(pj[0][:, i * P:(i + 1) * P], wks[:, i * P:(i + 1) * P], z[:, v, :, 0, :], start=True, stop=True)
                    mm.then_inc(ks_done, 1)
                if has(k):
                    for b in range(PER):
                        pe.wait_ge(k_lat, 2 * k + b + 1)
                        pe.matmul(pj[1 + b][:, :], z[:, v, b, :, :].rearrange("p c k -> p (c k)"), wv[:, :], start=True,
                                  stop=True).then_inc(v_done, 1)
                for b in range(PER):
                    if has(t):
                        pe.wait_ge(probs_ready, PER * t + b + 1)
                        if b > 0 or has(t - 1):
                            pe.wait_ge(pt_copied, PER * t + b)
                        for i in range(XU):
                            mm = pe.transpose(p_t[:, i * P:(i + 1) * P], pr[:, u % 2, b, i, :], g["ident"][:, :])
                        mm.then_inc(pt_done, 1)
                    if has(t + 1):
                        scores(t + 1, (u + 1) % 2, b)
                if has(t):
                    pe.wait_ge(v_ready, PER * (t + 1))
                    if has(t - 1):
                        pe.wait_ge(oT_copied, t)
                    pe.wait_ge(pt_copied, PER * (t + 1))
                    for b in range(PER):
                        for i in range(XU):
                            for h in range(2):
                                at = (2 * i + h) * XD
                                mm = pe.matmul(p_o[XD * h:XD * h + XD, i * P + b * S:i * P + (b + 1) * S], vv[:, u, b, at:at + XD],
                                               pT[:, u % 2, b, i, h * S:(h + 1) * S], start=True, stop=True)
                    mm.then_inc(pv_done, 1)
                if has(t - 1):
                    norm.pe_transpose(pe, t - 1, (u - 1) % 2, p_y[:, P:2 * P])
                if has(t):
                    pe.wait_ge(oT_copied, t + 1)
                    if has(t - 1):
                        pe.wait_ge(norm.copied, t)
                        pe.wait_ge(x_made, t)
                    for i in range(XU):
                        mm = pe.matmul(p_y[:, 0:D], oT[:, u % 2, i, :], wo[:, i, :], start=i == 0, stop=i == XU - 1)
                    mm.then_inc(y_done, 1)

            turns(pe, turn, first, last, R)

        @block.vector
        def _(dve):
            dve.memset(qblk[:, :, :, :, :, :], 0.0).then_inc(zeroed, 1)
            dve.wait_ge(consts_in, 16 * len(loads))

            def turn(t, u):
                k, v = t + 2, u % 2
                if has(k):
                    if has(k - 2):
                        dve.wait_ge(s_done, PER * (k - 1))
                    for i in range(2):
                        dve.wait_ge(k_done, 2 * k + i + 1)
                        dve.tensor_tensor(kT[:, v, 2 * i:2 * i + 2, :, 0, :].rearrange("p i b k -> p (i b) k"),
                                          pj[1 + i][:, :].rearrange("p (n c k) -> p n c k", c=2, k=S)[:, :, 0, :],
                                          row_bc(table[:, 0, :], 4), ALU.mult).then_inc(k_cos, 1)
                    dve.wait_ge(ks_done, k + 1)
                    if has(k - 1):
                        dve.wait_ge(k_ready, k)
                    dve.tensor_tensor(ksin[:, :, :], pj[0][:, :].rearrange("p (n k) -> p n k", k=S), row_bc(table[:, 1, :], XU * PER),
                                      ALU.mult).then_inc(k_sin, 1)
                    dve.wait_ge(k_cos, 2 * (k + 1))
                    dve.wait_ge(k_sin, k + 1)
                    ctx_keys = kT[:, v, :, :, 0, :].rearrange("p i b k -> p (i b) k")
                    dve.tensor_tensor(ctx_keys, ctx_keys, ksin[:, :, :], ALU.add).then_inc(k_ready, 1)
                if has(t - 1):
                    n = t - 1
                    x = g["xs"][:, bass.ds(n, 1), :].rearrange("p a d -> p (a d)")
                    dve.wait_ge(y_done, n + 1)
                    dve.tensor_tensor(x, p_y[:, 0:D], x, ALU.add).then_inc(x_made, 1)
                    norm.dve_stats(dve, n, n % 2 if isinstance(n, int) else (u - 1) % 2)
                k, v = t + 1, (u + 1) % 2
                for b in range(PER):
                    if has(k):
                        dve.wait_ge(s_done, PER * k + b + 1)
                        if has(k - 2):
                            dve.wait_ge(exped, XH * (k - 1))
                        dve.tensor_reduce(sm[:, v, b, 0, :], p_s[b][:, :].rearrange("p (i k) -> p i k", i=XU), AX, ALU.max,
                                          negate=True).then_inc(maxed, 1)
                    if b == 0 and has(t - 1):
                        norm.dve_norm(dve, t - 1, (u - 1) % 2)
                for b in range(PER):
                    if has(k):
                        dve.wait_ge(exped, XH * k + XU * (b + 1))
                        dve.reciprocal(sm[:, v, b, 2, :], sm[:, v, b, 1, :]).then_inc(inverted, 1)
                        dve.wait_ge(inverted, PER * k + b + 1)
                        dve.tensor_tensor(pr[:, v, b], pr[:, v, b], col_bc(sm[:, v, b, 2, :], K), ALU.mult).then_inc(probs_ready, 1)

            turns(dve, turn, first, last, R)

        @block.gpsimd
        def _(pool):
            def turn(t, u):
                k, v = t + 3, (u + 3) % 2
                if has(k):
                    if has(k - 2):
                        pool.wait_ge(v_done, PER * (k - 1))
                    for i, src in enumerate(("cnT", "xnT")):
                        pool.tensor_copy(z[:, v, :, i, :], g[src][:, bass.ds(k * P, P)].rearrange("p (b s) -> p b s", b=PER)).then_inc(z_ready, 1)
                if has(t - 1):
                    norm.pool_rstd(pool, t - 1, (u - 1) % 2)

            turns(pool, turn, first, last, R)

        @block.scalar
        def _(act):
            act.wait_ge(consts_in, 16 * len(loads))
            act.wait_ge(zeroed, 1)

            def turn(t, u):
                k, v = t + 2, u % 2
                if has(k):
                    act.wait_ge(q_done, k + 1)
                    if has(k - 2):
                        act.wait_ge(s_done, PER * (k - 1))
                    for h in range(2):
                        rows = slice(XD * h, XD * h + XD)
                        act.activation(qblk[rows, v, :, :, h, :].rearrange("p i b q -> p (i b) q"),
                                       pj[0][rows, :].rearrange("p (n q) -> p n q", q=S), ACT.Copy, scale=float(XD) ** -0.5).then_inc(q_ready, 1)
                    for i in range(2):
                        act.wait_ge(k_cos, 2 * k + i + 1)
                        act.activation(kT[:, v, 2 * i:2 * i + 2, :, 1, :].rearrange("p i b k -> p (i b) k"),
                                       pj[1 + i][:, :].rearrange("p (n c k) -> p n c k", c=2, k=S)[:, :, 1, :], ACT.Copy).then_inc(k_lat, 1)
                    if has(t - 2):
                        act.wait_ge(pv_done, t - 1)
                    for b in range(PER):
                        act.wait_ge(v_done, PER * k + b + 1)
                        act.activation(vv[:, (u + 2) % 4, b, :], pj[1 + b][:, :], ACT.Copy).then_inc(v_ready, 1)
                k, v = t + 1, (u + 1) % 2
                for b in range(PER):
                    if has(t):
                        act.wait_ge(pt_done, PER * t + b + 1)
                        if has(t - 2):
                            act.wait_ge(pv_done, t - 1)
                        act.activation(pT[:, u % 2, b].rearrange("p i k -> p (i k)"), p_t[:, :], ACT.Copy).then_inc(pt_copied, 1)
                if has(t):
                    act.wait_ge(pv_done, t + 1)
                    if has(t - 2):
                        act.wait_ge(y_done, t - 1)
                    act.activation(oT[:, u % 2].rearrange("p i q -> p (i q)"), p_o[:, :], ACT.Copy).then_inc(oT_copied, 1)
                if has(t - 1):
                    norm.act_copy(act, t - 1, p_y[:, P:2 * P])
                for b in range(PER):
                    if has(k):
                        act.wait_ge(maxed, PER * k + b + 1)
                        if has(k - 2):
                            act.wait_ge(pt_done, PER * (k - 2) + b + 1)
                        for i in range(XU):
                            act.activation(pr[:, v, b, i, :], p_s[b][:, i * K:(i + 1) * K], ACT.Exp, bias=sm[:, v, b, 0, i:i + 1],
                                           accum_out=sm[:, v, b, 1, i:i + 1]).then_inc(exped, 1)

            turns(act, turn, first, last, R)


SN, SP = 64, 32
CW = 512
CN = CW // SP
CQ = CW // P
CHUNKS = SN * SP // CW
LOWEST = -3e38


def soft_experts(nc, g, io, out):
    R = 4
    phi_d = io["L1_ffn_phi"].rearrange("d n p -> d (n p)").rearrange("d (c s) -> c d s", c=CHUNKS)
    w_d = io["w_soft"].rearrange("c d n e -> c d (n e)")
    b_d = io["L1_ffn_b"].rearrange("(c j i) e -> c i j e", c=CHUNKS, i=P // SP)
    with Mem(nc, "sm") as m:
        logits = m.sb("logits", [P, NT, CW])
        combT = m.sb("combT", [P, CQ, NT * P])
        acc = m.sb("acc", [P, NT, D])
        w = m.sb("w", [P, CN, D])
        wb = m.sb("wb", [P, CQ, D])
        peak = m.sb("peak", [P, CW])
        xg = m.sb("xg", [P, 2, P])
        nmax, nmax_new, rows = m.sb("nmax", [P, NT]), m.sb("nmax_new", [P, NT]), m.sb("rows", [P, NT])
        decay, total = m.sb("decay", [P, NT]), m.sb("total", [P, NT])
        state_set, phi_in, w_in = m.sem("state_set"), m.sem("phi_in"), m.sem("w_in")
        xg_copied, l_done, row_maxed, min_made, l_copied, exped = (
            m.sem(n) for n in ("xg_copied", "l_done", "row_maxed", "min_made", "l_copied", "exped"))
        rows_kept, peaked, ct_done, ct_copied = (m.sem(n) for n in ("rows_kept", "peaked", "ct_done", "ct_copied"))
        merged, fold_in, centred, d_exped, z_done, inverted = (
            m.sem(n) for n in ("merged", "fold_in", "centred", "d_exped", "z_done", "inverted"))
        decay_step = m.sem("decay_step")
        zeroed, xr_copied, cg_copied, xt_done, xz_ready, dn_ready = (
            m.sem(n) for n in ("zeroed", "xr_copied", "cg_copied", "xt_done", "xz_ready", "dn_ready"))
        s_done, s_copied, y_done, y_copied, o_done, acc_made = (
            m.sem(n) for n in ("s_done", "s_copied", "y_done", "y_copied", "o_done", "acc_made"))
        used = range(min(USED), max(USED) + 1)
        USED.clear()

        with nc.Block() as block:
            @block.vector
            def _(dve):
                dve.memset(nmax[:, :], -LOWEST)
                dve.memset(total[:, :], 0.0)
                dve.memset(acc[:, :, :], 0.0)

        with nc.Fori(0, CHUNKS) as c:
            with nc.Block() as block:
                @block.sync
                def _(sync):
                    sync.sem_clear(used)

            with Mem(nc, "sa") as ma:
                phi = ma.sb("phi", [P, CW])
                comb = ma.sb("comb", [P, 2, CW])
                small = ma.sb("small", [P, R, 3])
                p_l = [ma.ps(f"p_l{i}") for i in range(R)]
                p_e = [ma.ps(f"p_e{i}") for i in range(2)]
                with nc.Block() as block:
                    @block.gpsimd
                    def _(pool):
                        def turn(t, u):
                            k, v = t + 3, (u + 3) % 2
                            if has(k):
                                if has(k - 2):
                                    pool.wait_ge(l_done, k - 1)
                                pool.tensor_copy(xg[:, v, :], g["xnT"][:, bass.ds(k * P, P)]).then_inc(xg_copied, 1)

                        turns(pool, turn, -3, NT, R)

                    @block.tensor
                    def _(pe):
                        pe.wait_ge(phi_in, 16)

                        def turn(t, u):
                            k, v = t + 2, (u + 2) % R
                            if has(k):
                                pe.wait_ge(xg_copied, k + 1)
                                if has(k - R):
                                    pe.wait_ge(exped, k - R + 1)
                                pe.matmul(p_l[v][:, :], xg[:, v % 2, :], phi[:, :], start=True, stop=True).then_inc(l_done, 1)
                            if has(t):
                                pe.wait_ge(exped, t + 1)
                                if has(t - 2):
                                    pe.wait_ge(ct_copied, t - 1)
                                for j in range(CQ):
                                    mm = pe.transpose(p_e[u % 2][:, j * P:(j + 1) * P], comb[:, u % 2, j * P:(j + 1) * P], g["ident"][:, :])
                                mm.then_inc(ct_done, 1)

                        turns(pe, turn, -2, NT, R)

                    @block.vector
                    def _(dve):
                        dve.memset(peak[:, :], LOWEST).then_inc(peaked, 1)

                        def turn(t, u):
                            k, v = t + 1, (u + 1) % R
                            if has(k):
                                dve.wait_ge(l_done, k + 1)
                                dve.tensor_reduce(small[:, v, 0:1], p_l[v][:, :], AX, ALU.max, negate=True).then_inc(row_maxed, 1)
                                dve.wait_ge(row_maxed, k + 1)
                                if has(k - R):
                                    dve.wait_ge(exped, k - R + 1)
                                dve.tensor_tensor(small[:, v, 1:2], nmax[:, bass.ds(k, 1)], small[:, v, 0:1], ALU.min).then_inc(min_made, 1)
                            if has(t):
                                dve.wait_ge(l_copied, t + 1)
                                dve.wait_ge(peaked, t + 1)
                                dve.tensor_tensor(peak[:, :], peak[:, :], logits[:, bass.ds(t, 1), :].rearrange("p a s -> p (a s)"),
                                                  ALU.max).then_inc(peaked, 1)
                                dve.wait_ge(exped, t + 1)
                                dve.tensor_copy(nmax_new[:, bass.ds(t, 1)], small[:, u, 1:2]).then_inc(rows_kept, 1)
                                dve.tensor_copy(rows[:, bass.ds(t, 1)], small[:, u, 2:3]).then_inc(rows_kept, 1)

                        turns(dve, turn, -1, NT, R)

                    @block.scalar
                    def _(act):
                        act.dma_start(phi[:, :], phi_d[bass.ds(c, 1), :, :].rearrange("a d s -> d (a s)")).then_inc(phi_in, 16)
                        act.dma_start(w[:, :, :].rearrange("p n e -> p (n e)"), w_d[bass.ds(c, 1), :, :].rearrange("a d m -> d (a m)")).then_inc(w_in, 16)
                        for i in range(P // SP):
                            act.dma_start(wb[SP * i:SP * (i + 1), :, :],
                                          b_d[bass.ds(c, 1), i, :, :].to_broadcast([SP, CQ, D])).then_inc(w_in, 16)

                        def turn(t, u):
                            act.wait_ge(min_made, t + 1)
                            act.activation(logits[:, bass.ds(t, 1), :].rearrange("p a s -> p (a s)"), p_l[u][:, :], ACT.Copy).then_inc(l_copied, 1)
                            if has(t - 2):
                                act.wait_ge(ct_done, t - 1)
                            if has(t - R):
                                act.wait_ge(rows_kept, 2 * (t - R + 1))
                            act.activation(comb[:, u % 2, :], p_l[u][:, :], ACT.Exp, bias=small[:, u, 1:2],
                                           accum_out=small[:, u, 2:3]).then_inc(exped, 1)

                        def turn_and_last(t, u):
                            if has(t):
                                turn(t, u)
                            if has(t - 1):
                                act.wait_ge(ct_done, t)
                                act.activation(combT[:, :, bass.ds((t - 1) * P, P)],
                                               p_e[(u - 1) % 2][:, :].rearrange("p (j q) -> p j q", j=CQ), ACT.Copy).then_inc(ct_copied, 1)

                        turns(act, turn_and_last, 0, NT + 1, R)

            with Mem(nc, "sz") as mz:
                fold = mz.sb("fold", [P, P])
                other = mz.sb("other", [S, CW])
                p_z = mz.ps("p_z")
                with nc.Block() as block:
                    @block.sync
                    def _(sync):
                        sync.dma_start(fold[:, :], io["c_fold"]).then_inc(fold_in, 16)

                    @block.vector
                    def _(dve):
                        dve.tensor_copy(other[:, :], peak[S:P, :]).then_inc(merged, 1)
                        dve.wait_ge(merged, 1)
                        dve.tensor_tensor(peak[0:S, :], peak[0:S, :], other[:, :], ALU.max).then_inc(merged, 1)
                        dve.wait_ge(merged, 2)
                        dve.tensor_copy(peak[S:P, :], peak[0:S, :]).then_inc(merged, 1)
                        dve.wait_ge(merged, 3)

                        def turn(t, u):
                            at = logits[:, bass.ds(t, 1), :].rearrange("p a s -> p (a s)")
                            dve.tensor_tensor(at, at, peak[:, :], ALU.subtract).then_inc(centred, 1)

                        turns(dve, turn, 0, NT, R)
                        dve.wait_ge(z_done, 1)
                        dve.reciprocal(peak[:, :], p_z[:, :])
                        dve.tensor_tensor(decay[:, :], nmax_new[:, :], nmax[:, :], ALU.subtract).then_inc(decay_step, 1)
                        dve.wait_ge(decay_step, 2)
                        dve.tensor_copy(nmax[:, :], nmax_new[:, :])
                        dve.tensor_tensor(total[:, :], total[:, :], decay[:, :], ALU.mult).then_inc(decay_step, 1)
                        dve.wait_ge(decay_step, 3)
                        dve.tensor_tensor(total[:, :], total[:, :], rows[:, :], ALU.add)

                    @block.scalar
                    def _(act):
                        def turn(t, u):
                            act.wait_ge(centred, t + 1)
                            at = logits[:, bass.ds(t, 1), :].rearrange("p a s -> p (a s)")
                            act.activation(at, at, ACT.Exp).then_inc(d_exped, 1)

                        turns(act, turn, 0, NT, R)
                        act.wait_ge(decay_step, 1)
                        act.activation(decay[:, :], decay[:, :], ACT.Exp).then_inc(decay_step, 1)

                    @block.tensor
                    def _(pe):
                        pe.wait_ge(fold_in, 16)

                        def turn(t, u):
                            pe.wait_ge(d_exped, t + 1)
                            static = isinstance(t, int)
                            mm = pe.matmul(p_z[:, :], fold[:, :], logits[:, bass.ds(t, 1), :].rearrange("p a s -> p (a s)"),
                                           start=static and t == 0, stop=static and t == NT - 1)
                            if static and t == NT - 1:
                                mm.then_inc(z_done, 1)

                        turns(pe, turn, 0, NT, R)

            with Mem(nc, "sc") as mc:
                xz = mc.sb("xz", [P, 2, PER, D])
                sT = mc.sb("sT", [P, PER, CW])
                yy = mc.sb("yy", [P, PER, CQ, D])
                cg = mc.sb("cg", [P, 2, CQ, P])
                p_x = mc.ps("p_x")
                p_s = [mc.ps(f"p_s{i}") for i in range(PER)]
                p_y = [mc.ps(f"p_y{i}") for i in range(PER)]
                p_o = [mc.ps(f"p_o{i}") for i in range(2)]
                with nc.Block() as block:
                    @block.gpsimd
                    def _(pool):
                        def turn(t, u):
                            k, v = t + 4, u % 2
                            if has(k):
                                if has(k - 2):
                                    pool.wait_ge(xt_done, k - 1)
                                pool.tensor_copy(xg[:, v, :], g["xnT"][:, bass.ds(k * P, P)]).then_inc(xr_copied, 1)
                            k, v = t + 1, (u + 1) % 2
                            if has(k):
                                if has(k - 2):
                                    pool.wait_ge(o_done, PER * (k - 1))
                                pool.tensor_copy(cg[:, v, :, :], combT[:, :, bass.ds(k * P, P)]).then_inc(cg_copied, 1)

                        turns(pool, turn, -4, NT, R)

                    @block.tensor
                    def _(pe):
                        pe.wait_ge(w_in, 16 * (1 + P // SP))
                        pe.wait_ge(zeroed, 1)

                        def turn(t, u):
                            k, v = t + 3, (u + 3) % 2
                            if has(k):
                                pe.wait_ge(xr_copied, k + 1)
                                if has(k - 1):
                                    pe.wait_ge(xz_ready, PER * k)
                                pe.transpose(p_x[:, 0:D], xg[:, v, :], g["ident"][:, :]).then_inc(xt_done, 1)
                            k, v = t + 2, u % 2
                            if has(k):
                                pe.wait_ge(xz_ready, PER * (k + 1))
                                pe.wait_ge(dn_ready, k + 1)
                                for b in range(PER):
                                    if has(k - 1):
                                        pe.wait_ge(s_copied, PER * (k - 1) + b + 1)
                                    pe.matmul(p_s[b][:, :], xz[:, v, b, :], logits[:, bass.ds(k, 1), :].rearrange("p a s -> p (a s)"),
                                              start=True, stop=True).then_inc(s_done, 1)
                            k = t + 1
                            if has(k):
                                for b in range(PER):
                                    pe.wait_ge(s_copied, PER * k + b + 1)
                                    if has(k - 1):
                                        pe.wait_ge(y_copied, PER * (k - 1) + b + 1)
                                    for j in range(CQ):
                                        for i in range(P // SP):
                                            n = (P // SP) * j + i
                                            mm = pe.matmul(p_y[b][SP * i:SP * (i + 1), j * D:(j + 1) * D], sT[:, b, n * SP:(n + 1) * SP],
                                                           w[:, n, :], start=True, stop=True)
                                    mm.then_inc(y_done, 1)
                            if has(t):
                                pe.wait_ge(cg_copied, t + 1)
                                if has(t - 2):
                                    pe.wait_ge(acc_made, t - 1)
                                for b in range(PER):
                                    pe.wait_ge(y_copied, PER * t + b + 1)
                                    for j in range(CQ):
                                        mm = pe.matmul(p_o[u % 2][b * S:(b + 1) * S, 0:D], cg[:, u % 2, j, b * S:(b + 1) * S],
                                                       yy[:, b, j, :], start=j == 0, stop=j == CQ - 1)
                                    mm.then_inc(o_done, 1)

                        turns(pe, turn, -3, NT, R)

                    @block.vector
                    def _(dve):
                        dve.memset(xz[:, :, :, :], 0.0).then_inc(zeroed, 1)
                        dve.wait_ge(w_in, 16 * (1 + P // SP))

                        def turn(t, u):
                            k = t + 3
                            if has(k):
                                at = logits[:, bass.ds(k, 1), :].rearrange("p a s -> p (a s)")
                                dve.tensor_tensor(at, at, peak[:, :], ALU.mult).then_inc(dn_ready, 1)
                            if has(t):
                                dve.wait_ge(o_done, PER * (t + 1))
                                at = acc[:, bass.ds(t, 1), :].rearrange("p a d -> p (a d)")
                                dve.scalar_tensor_tensor(at, at, decay[:, bass.ds(t, 1)], p_o[u % 2][:, 0:D], ALU.mult, ALU.add).then_inc(acc_made, 1)
                            k = t + 1
                            if has(k):
                                for b in range(PER):
                                    dve.wait_ge(y_done, PER * k + b + 1)
                                    dve.tensor_tensor(yy[:, b, :, :].rearrange("p j e -> p (j e)"), p_y[b][:, :],
                                                      wb[:, :, :].rearrange("p j e -> p (j e)"), ALU.add).then_inc(y_copied, 1)

                        turns(dve, turn, -3, NT, R)

                    @block.scalar
                    def _(act):
                        act.wait_ge(zeroed, 1)

                        def turn(t, u):
                            k, v = t + 3, (u + 3) % 2
                            if has(k):
                                act.wait_ge(xt_done, k + 1)
                                if has(k - 2):
                                    act.wait_ge(s_done, PER * (k - 1))
                                for b in range(PER):
                                    half = slice(b * S, (b + 1) * S)
                                    act.activation(xz[half, v, b, :], p_x[half, 0:D], ACT.Copy).then_inc(xz_ready, 1)
                            k = t + 2
                            if has(k):
                                for b in range(PER):
                                    act.wait_ge(s_done, PER * k + b + 1)
                                    if has(k - 1):
                                        act.wait_ge(y_done, PER * (k - 1) + b + 1)
                                    act.activation(sT[:, b, :], p_s[b][:, :], ACT.Copy).then_inc(s_copied, 1)

                        turns(act, turn, -3, NT, R)

        PIECES = 4
        n = NT // PIECES
        made, stored = m.sem("made"), m.sem("stored")
        out_d = out.rearrange("(t b) s d -> (b s) t d", b=PER)
        USED.clear()
        with nc.Block() as block:
            @block.vector
            def _(dve):
                dve.reciprocal(total[:, :], total[:, :]).then_inc(made, 1)
                dve.wait_ge(made, 1)
                for i in range(PIECES):
                    at = slice(i * n, (i + 1) * n)
                    dve.tensor_tensor(acc[:, at, :], acc[:, at, :], col_bc(total[:, at], D), ALU.mult).then_inc(made, 1)
                    dve.wait_ge(made, 2 * i + 2)
                    dve.tensor_tensor(g["xs"][:, at, :], g["xs"][:, at, :], acc[:, at, :], ALU.add).then_inc(made, 1)

            @block.sync
            def _(sync):
                for i in range(PIECES):
                    at = slice(i * n, (i + 1) * n)
                    sync.wait_ge(made, 2 * i + 3)
                    sync.dma_start(out_d[:, at, :], g["xs"][:, at, :]).then_inc(stored, 16)
                sync.wait_ge(stored, 16 * PIECES)


def program(nc, io, out):
    USED.clear()
    with Mem(nc, "g") as m:
        g = {}
        g["ident"] = m.sb("ident", [P, P])
        g["gbx"] = m.sb("gbx", [P, 2])
        g["gbl"] = m.sb("gbl", [P, 2])
        g["neghalf"] = m.sb("neghalf", [P, 4])
        g["eps"] = m.sb("eps", [P, 4])
        g["gate"] = m.sb("gate", [P, GATES])
        g["carries"] = 0
        g["xs"] = m.sb("xs", [P, NT, D])
        g["xnT"] = m.sb("xnT", [P, NT * P])
        with Mem(nc, "early") as early:
            g["ctxT"] = early.sb("ctxT", [P, NT * P])
            g["cnT"] = early.sb("cnT", [P, NT * P])
            load_and_norm(nc, g, io)
            attention(nc, g, io, 0)
            mlstm(nc, g, io)
            experts(nc, g, io)
            attention(nc, g, io, 1)
            clear_semaphores(nc)
            cross_attention(nc, g, io)
        soft_experts(nc, g, io, out)


def shape_constants():
    p = np.arange(P)
    k = np.arange(S)
    later = k[None, :] > (p % S)[:, None]
    c = {"c_ident": np.eye(P)}
    c["c_heads"] = (p // HD)[:, None] == np.arange(NH)[None, :]
    c["c_causal"] = np.where(later, -1e9, 0.0)
    slopes = (2.0 ** (-8.0 * np.arange(1, NH + 1) / NH)).astype(np.float32)
    alike = (p // S)[:, None] == (p // S)[None, :]
    c["c_same"] = alike
    c["c_tri"] = alike & (p[:, None] <= p[None, :])
    c["c_diag"] = (p % S)[:, None] == k[None, :]
    inv = np.float32(1) / np.float32(10000) ** (np.arange(0, HD, 2, dtype=np.float32) / np.float32(HD))
    angle = (k.astype(np.float32)[None, :] * inv[(p % HD) // 2][:, None]).astype(np.float32)
    sign = np.where(p % 2 == 0, -1.0, 1.0)[:, None]
    cos, sin, scale = np.cos(angle), np.sin(angle) * sign, float(HD) ** -0.5
    c["c_rope8"] = np.concatenate([cos * scale, sin * scale, cos, sin], 1)
    inv = np.float32(1) / np.float32(10000) ** (np.arange(0, XD, 2, dtype=np.float32) / np.float32(XD))
    angle = (k.astype(np.float32)[None, :] * inv[p % (XD // 2)][:, None]).astype(np.float32)
    sign = np.where(p % XD < XD // 2, -1.0, 1.0)[:, None]
    c["c_rope64"] = np.concatenate([np.cos(angle), np.sin(angle) * sign], 1)
    c["c_seg"] = np.broadcast_to(np.arange(4 * NE) % NE != 0, (P, 4 * NE))
    c["c_fold"] = (p % S)[:, None] == (p % S)[None, :]
    c = {n: v.astype(np.float32) for n, v in c.items()}
    bf16 = mybir.dt.np(BF16)
    spread = np.zeros((P, NE, P))
    for e in range(NE):
        spread[[e, NE + e, 2 * NE + e], e] = 1.0
    c["c_spread"] = spread.reshape(P, NE * P).astype(bf16)
    c["c_identb"] = np.eye(P).astype(bf16)
    pick = np.zeros((P, P), np.float32)
    pick[p % S, p] = 1.0
    pick[S:S + 3] = 1.0
    pick[S + 3:S + 6] = p % S
    c["c_pick"] = pick.astype(bf16)
    for layer, low in ((0, -1e9), (1, -1e30)):
        bias = np.zeros((P, NH, S), np.float32)
        bias[:S] = np.where(later[:S], low, 0.0)[:, None, :]
        if layer:
            for row, rest in ((S, slopes[:, None] * k.astype(np.float32)), (S + 3, np.broadcast_to(-slopes[:, None], (NH, S)))):
                for part in range(3):
                    bias[row + part] = rest.astype(bf16).astype(np.float32)
                    rest = rest - bias[row + part]
        c[f"c_bias{layer}"] = bias.reshape(P, NH * S).astype(bf16)
    return c


def kernel(**inputs):
    import concourse.bacc as bacc
    from concourse.bass_utils import run_bass_kernel_spmd

    a = {k: np.asarray(v) for k, v in inputs.items()}
    arrays = {"x": a["x"], "ctx_1024": a["ctx_1024"]}
    arrays["w_gbx"] = np.stack([a["L1_xattn_gamma_x"], a["L1_xattn_beta_x"]], 1)
    arrays["w_gbl"] = np.stack([a["L1_xattn_gamma_l"], a["L1_xattn_beta_l"]], 1)
    swap = np.arange(D) ^ 1
    for n in ("wq", "wk", "wv", "wo"):
        arrays["w0_" + n] = a["L0_attn_" + n]
        arrays["w1_" + n] = a["L1_attn_W" + n[1]].T
    arrays["w0_wqs"], arrays["w0_wks"] = a["L0_attn_wq"][:, swap], a["L0_attn_wk"][:, swap]
    bq, bk = a["L0_attn_bq"], a["L0_attn_bk"]
    arrays["w0_cols"] = np.stack([bq, bq[swap], bk, bk[swap], a["L0_attn_bv"]], 1)
    arrays["w0_bo"] = a["L0_attn_bo"]
    arrays["w_mgates"] = np.concatenate([a["L0_xattn_igate_kernel"], a["L0_xattn_fgate_kernel"]], 1)
    arrays["w_mbias"] = np.concatenate([a["L0_xattn_igate_bias"], a["L0_xattn_fgate_bias"]])
    arrays["w_mscale"] = a["L0_xattn_outnorm_scale"]
    arrays["w_b1"] = np.concatenate([a["L0_ffn_sb1"].reshape(CS, P), a["L0_ffn_rb1"].reshape(NE * CE, P)]).T
    arrays["w_b2"] = np.concatenate([a["L0_ffn_rb2"], a["L0_ffn_sb2"]])
    for n in ("L0_ffn_gW", "L0_ffn_gb", "L0_ffn_sW1", "L0_ffn_sW2", "L0_ffn_rW1", "L0_ffn_rW2"):
        arrays[n] = a[n]
    half = np.arange(XH * XD) ^ (XD // 2)
    wkv = a["L1_xattn_Wkv"]
    arrays["w_xk"], arrays["w_xks"], arrays["w_xv"] = wkv[:, :XH * XD], wkv[:, half], wkv[:, XH * XD:]
    arrays["L1_xattn_Wq"], arrays["L1_xattn_Wo"] = a["L1_xattn_Wq"], a["L1_xattn_Wo"]
    arrays["L1_ffn_phi"], arrays["L1_ffn_b"] = a["L1_ffn_phi"], a["L1_ffn_b"]
    arrays["w_soft"] = a["L1_ffn_W"].reshape(CHUNKS, CN, D, D).transpose(0, 2, 1, 3)
    arrays.update(shape_constants())
    arrays = {k: np.ascontiguousarray(v) for k, v in arrays.items()}
    nc = bacc.Bacc("TRN2", target_bir_lowering=False, num_devices=1)
    io = {k: nc.dram_tensor("in_" + k, v.shape, mybir.dt.from_np(v.dtype), kind="ExternalInput").ap() for k, v in arrays.items()}
    out = nc.dram_tensor("out_x", (B, S, D), F32, kind="ExternalOutput").ap()
    program(nc, io, out)
    r = run_bass_kernel_spmd(nc, [{"in_" + k: v for k, v in arrays.items()}], core_ids=[0])
    return r.results[0]["out_x"]
```
